# Optimizing a Trainium2 kernel written in Bass

```python
import numpy as np
import jax
import jax.numpy as jnp

def _softmax(x, axis=-1):
    return jax.nn.softmax(x, axis=axis)
def _gelu(x):
    return jax.nn.gelu(x, approximate=True)
def _silu(x):
    return jax.nn.silu(x)
def _sigmoid(x):
    return jax.nn.sigmoid(x)
def _layernorm(x, axis=-1, eps=1e-5):
    m = jnp.mean(x, axis=axis, keepdims=True)
    v = jnp.var(x, axis=axis, keepdims=True)
    return (x - m) / jnp.sqrt(v + eps)
def _scatter_add(tgt, idx, src, axis=0):
    return tgt.at[idx].add(src)
def _segment_sum(src, seg, n):
    return jax.ops.segment_sum(src, seg, n)

kernel_name = 'mk_adj_resnorm_d1_adj_256_2992c4'

def setup_inputs(seed: int = 0):
    np.random.seed(seed)
    _w = jnp.asarray
    def _rec_inputs():
        import jax
        import jax.numpy as jnp
        _gk = jax.random.key(seed)
        x = -0.000929 + 1 * jax.random.normal(jax.random.fold_in(_gk, 1), (8192, 256), jnp.float32)
        _a = jax.random.bernoulli(jax.random.fold_in(_gk, 2), 0.000976562, (8192, 8192))
        _a = jnp.logical_or(_a, jnp.swapaxes(_a, -1, -2))
        _a = jnp.logical_or(_a, jnp.eye(8192, dtype=bool))
        adj = _a.astype(jnp.int32)
        return x, adj
    x, adj = _rec_inputs()
    def _L0_gnn_setup():
        import jax, jax.numpy as jnp
        import numpy as np
        N = 4096
        IN_F = 256
        OUT_F = 64
        HEADS = 4
        NEG_SLOPE = 0.2
        key = jax.random.key(seed)
        k1, k2, k3, k4 = jax.random.split(key, 4)
        x = jax.random.normal(k1, (N, IN_F), dtype=jnp.float32)
        W = jax.random.normal(k2, (HEADS, IN_F, OUT_F), dtype=jnp.float32) * (1.0 / np.sqrt(IN_F))
        a = jax.random.normal(k3, (HEADS, 2 * OUT_F), dtype=jnp.float32) * (1.0 / np.sqrt(2 * OUT_F))
        adj_matrix = jax.random.randint(k4, (N, N), 0, 2, dtype=jnp.int32)
        return {'x': x, 'W': W, 'a': a, 'adj_matrix': adj_matrix}
    _L0_gnn_all = _L0_gnn_setup()
    _L0_gnn_in = {k: v for k, v in _L0_gnn_all.items() if k in ('W', 'a', )}
    del _L0_gnn_all

    return {
        "x": x,
        "adj": adj,
        "L0_gnn_W": _L0_gnn_in["W"],
        "L0_gnn_a": _L0_gnn_in["a"],
    }

def reference(x, adj, L0_gnn_W, L0_gnn_a):
    import jax
    import jax.numpy as jnp
    def _L0_gnn_ref(x, W, a, adj_matrix):
        import jax, jax.numpy as jnp
        import numpy as np
        N = 4096
        IN_F = 256
        OUT_F = 64
        HEADS = 4
        NEG_SLOPE = 0.2
        heads, in_f, out_f = W.shape
        n = x.shape[0]
        xt = jnp.einsum('ni,hio->hno', x, W)
        src = jnp.einsum('hnf,hf->hn', xt, a[:, :out_f])
        dst = jnp.einsum('hnf,hf->hn', xt, a[:, out_f:])
        e = jax.nn.leaky_relu(src[:, :, None] + dst[:, None, :], NEG_SLOPE)
        mask = (adj_matrix > 0)[None, :, :]
        e = jnp.where(mask, e, -jnp.inf)
        attention = jax.nn.softmax(e, axis=2)
        h_prime = jnp.einsum('hij,hjf->hif', attention, xt)
        return h_prime.transpose(1, 0, 2).reshape(n, heads * out_f)

    x = _layernorm(x + _L0_gnn_ref(x, L0_gnn_W, L0_gnn_a, adj), axis=-1)
    return x


_drawn_inputs = setup_inputs


def setup_inputs(seed=0):
    import zlib

    import numpy as np

    out = dict(_drawn_inputs(seed))
    spreads = {}
    factors = {}
    for name, (base, spread) in spreads.items():
        noise = np.random.default_rng([zlib.crc32(name.encode()), seed]).standard_normal(out[name].shape)
        drawn = base * np.exp(spread * noise) if base else spread * noise
        out[name] = jnp.asarray(drawn.astype(out[name].dtype))
    for name, factor in factors.items():
        out[name] = (out[name] * factor).astype(out[name].dtype)
    return out
```

```python
import concourse.bass as bass
from concourse import mybir
from contextlib import ExitStack



def gat_residual_norm(nc: bass.Bass, x: bass.AP, adj: bass.AP, W: bass.AP, a: bass.AP, out: bass.AP):
    fp32 = mybir.dt.float32
    fp16 = mybir.dt.float16
    fp8 = mybir.dt.float8e4
    u32 = mybir.dt.uint32
    i32 = mybir.dt.int32
    i8 = mybir.dt.int8
    u8 = mybir.dt.uint8
    ALU = mybir.AluOpType
    ACT = mybir.ActivationFunctionType
    AX = mybir.AxisListType
    RMAX = bass.bass_isa.ReduceOp.max

    P = 128
    N, F = x.shape
    H, _, O = W.shape
    B = 4
    CW = B * P
    NC = N // CW
    NG = N // CW
    R = N // P
    KF = F // P
    VO = O + 1
    HV = 4 * VO
    VW = H * HV
    VX = VW // 2
    HP = 2
    NP = NC * (H // HP)
    WX = F + 2 * H
    SLOPE = 0.2
    EPS = 1e-5
    LOW = 2.0 ** 14
    QUEUE = 4 * HP * B
    assert N % CW == 0 and F == KF * P and H == 4 and H * O == F and QUEUE == 32
    HALF = NG // 2
    SP_ = 2 * NG

    ctx = ExitStack()
    with ctx:
        def sb(name, shape, dt):
            return ctx.enter_context(nc.sbuf_tensor(name, shape, dt))

        def sem(name):
            return ctx.enter_context(nc.semaphore(name))

        V = sb("V", [P, R * VW], fp16)
        V32 = V[:, :].bitcast(fp32)
        AT = sb("AT", [P, NG * CW], u32)
        raw = sb("raw", [P, B, CW], i32)
        nat = sb("nat", [P, B, CW], u8)
        srow = sb("srow", [P, 2, HP, CW], fp32)
        sgn = sb("sgn", [P, HP, CW, B], i8)
        pos = sb("pos", [P, HP, CW, B], fp8)
        neg = sb("neg", [P, HP, CW, B], fp8)
        u = sb("u", [P, HP, B, 2, VO], fp32)
        y = sb("y", [P, B, F], fp32)
        tab = sb("tab", [P, R, 2 * H], fp32)
        ab = sb("ab", [P, R, H, 2], fp32)
        ident = sb("ident", [P, P], fp32)
        mx = sb("mx", [P, H], fp32)
        M = sb("M", [P, H], fp32)
        rden = sb("rden", [P, HP, B], fp32)
        stats = sb("stats", [P, B, 6], fp32)
        mv = sb("mv", [P, B, 2], fp32)
        rstd = sb("rstd", [P, B], fp32)
        half = sb("half", [P, B], fp32)

        late = AT[:, HALF * CW:NG * CW].bitcast(fp32)
        xg = [late[:, n * B * F:(n + 1) * B * F].rearrange("p (b f) -> p b f", b=B) for n in range(2)]
        xT = [late[:, (2 + n) * B * F:(3 + n) * B * F].rearrange("p (k b q) -> p k b q", k=KF, b=B) for n in range(2)]
        UW = B * H * VO
        U1 = [late[:, n * UW:(n + 1) * UW].rearrange("p (r v) -> p r v", v=VO) for n in range(2)]
        masks = [m[:, :, :, :].rearrange("p h i b -> p (h i b)").bitcast(fp32) for m in (sgn, pos, neg)]
        Wx = y[:, :, :].rearrange("p b f -> p (b f)")[:, 0:KF * WX].rearrange("p (k n) -> p k n", k=KF)
        aB = masks[0][:, 0:H * 2 * O].rearrange("p (h n) -> p h n", h=H)
        prod = masks[1][:, 0:KF * F].rearrange("p (k h o) -> p k h o", k=KF, h=H)
        dM = masks[2][:, 0:R * H].rearrange("p (r h) -> p r h", h=H)
        tM = masks[2][:, R * H:2 * R * H].rearrange("p (r h) -> p r h", h=H)
        tN = masks[2][:, 2 * R * H:3 * R * H].rearrange("p (r h) -> p r h", h=H)
        tP = masks[2][:, 3 * R * H:4 * R * H].rearrange("p (r h) -> p r h", h=H)
        e1 = masks[0][:, 0:R * H].rearrange("p (r h) -> p r h", h=H)
        e2 = masks[0][:, R * H:2 * R * H].rearrange("p (r h) -> p r h", h=H)
        uall = u[:, :, :, :, :].rearrange("p h b c v -> p (h b c v)")
        U2 = [uall.rearrange("p (r v) -> p r v", v=VO), late[:, 2 * UW:3 * UW].rearrange("p (r v) -> p r v", v=VO)]
        sT = masks[1][0:R, 0:H * P].rearrange("r (h p) -> r h p", h=H)

        acc = ctx.enter_context(nc.psum_tensor("acc", [P, 6, 512], fp32))
        tp = ctx.enter_context(nc.psum_tensor("tp", [P, 512], fp32))
        spare = ctx.enter_context(nc.psum_tensor("spare", [P, 512], fp32))

        s_dram = nc.dram_tensor("s_rows", [H, N], fp32, kind="Internal").ap()

        w_in = sem("w_in")
        a_in = sem("a_in")
        x_in = [sem("x_in0"), sem("x_in1")]
        ident_set = sem("ident_set")
        prod_done = sem("prod_done")
        wx_done = sem("wx_done")
        xTp_done = sem("xTp_done")
        xT_done = sem("xT_done")
        xt_done = sem("xt_done")
        xt_kept = sem("xt_kept")
        mx_done = sem("mx_done")
        M_done = sem("M_done")
        exp_in = sem("exp_in")
        exp_done = sem("exp_done")
        scaled = sem("scaled")
        sTp_done = sem("sTp_done")
        sT_done = sem("sT_done")
        s_out = sem("s_out")
        negd_done = sem("negd_done")
        U1_done = sem("U1_done")
        U2_done = sem("U2_done")
        hi_done = sem("hi_done")
        lo_done = sem("lo_done")
        raw_in = [sem(f"raw_in{t}") for t in range(B)]
        conv_done = sem("conv_done")
        tp_done = sem("tp_done")
        at_done = sem("at_done")
        row_in = [[sem(f"row_in{q}{h}") for h in range(HP)] for q in range(2)]
        third_done = sem("third_done")
        sgn_done = sem("sgn_done")
        neg_done = sem("neg_done")
        pos_done = sem("pos_done")
        sums_done = sem("sums_done")
        low_done = sem("low_done")
        u_done = sem("u_done")
        wu_done = sem("wu_done")
        t_done = sem("t_done")
        rden_done = sem("rden_done")
        tr_done = sem("tr_done")
        y_done = sem("y_done")
        res_in = sem("res_in")
        stats_done = sem("stats_done")
        mv_done = sem("mv_done")
        pow_done = sem("pow_done")
        norm_done = sem("norm_done")
        out_done = sem("out_done")
        pe_passed = sem("pe_passed")
        pool_passed = sem("pool_passed")
        dve_passed = sem("dve_passed")

        block = ctx.enter_context(nc.Block())

        adj_v = adj.rearrange("(c p t) (g w) -> c g p t w", p=P, t=B, w=CW)
        x_v = x.rearrange("(g p b) f -> g p b f", p=P, b=B)
        out_v = out.rearrange("(g p b) f -> g p b f", p=P, b=B)
        s_v = s_dram.rearrange("h (c w) -> h c w", w=CW)

        def word(t, h):
            return t[:, h, :, :].rearrange("p i b -> p (i b)").bitcast(u32)

        def slot(t, cd):
            q = t * 2 + cd
            return q // 3, (q % 3) * 2 * VO

        def xt_of(g):
            return V32[:, bass.ds(g * (B * VX), B * VX)].rearrange("p (b n) -> p b n", b=B)[:, :, 0:F] \
                .rearrange("p b (h o) -> p b h o", h=H)

        def e_of(e, g):
            return e[:, bass.ds(g * B, B), :].unsqueeze(3).broadcast_to([P, B, H, O])

        def e_flat(e, g):
            return e[:, bass.ds(g * B, B), :].rearrange("p b h -> p (b h)")

        def V_part(g, part):
            return V[:, bass.ds(g * (B * VW), B * VW)].rearrange("p (r n) -> p r n", n=HV)[:, :, part * VO:(part + 1) * VO]

        tabf = tab[:, :, :].rearrange("p r n -> p (r n)")

        def acc_part(h, rect, part):
            if rect == 0:
                v = acc[:, 3 * h:3 * h + 2, 0:3 * 2 * VO].rearrange("p k (s n) -> p k s n", s=3)
                return v[:, :, :, part * VO:(part + 1) * VO]
            v = acc[:, 3 * h + 2, 0:2 * 2 * VO].rearrange("p (s n) -> p s n", s=2)
            return v[:, :, part * VO:(part + 1) * VO]


        @block.sync
        def _(sp):
            for k in range(KF):
                sp.dma_start(Wx[:, k, 0:F].rearrange("p (h o) -> p h o", h=H),
                             W[:, k * P:(k + 1) * P, :].rearrange("h p o -> p h o")).then_inc(w_in, 16)
            sp.dma_start(aB, a.rearrange("(q h) n -> q h n", q=1).broadcast_to([P, H, 2 * O])).then_inc(a_in, 16)
            with sp.Fori(0, NG // 2) as i:
                for n in range(2):
                    sp.wait_ge(xTp_done, 2 * i + n + 1)
                    sp.dma_start(xg[n], x_v[2 * i + n]).then_inc(x_in[n], 16)

            def load(c, g, k):
                for t in range(B):
                    sp.wait_ge(conv_done, 4 * k + t + 1)
                    sp.dma_start(raw[:, t, :], adj_v[c, g, :, t, :]).then_inc(raw_in[t], 16)

            def load_rows(c, p, q):
                for h in range(HP):
                    sp.dma_start(srow[:, q, h, :], s_v[HP * p + h, c].partition_broadcast(P)).then_inc(row_in[q][h], 16)

            with sp.Fori(0, HALF) as g:
                load(0, g, g)
            sp.wait_ge(s_out, 16)
            sp.wait_ge(lo_done, NG)
            load_rows(0, 0, 0)

            def one_pass(c, p):
                def group(j):
                    if p == 0:
                        load(c, HALF + j, NG * c + HALF + j)
                    else:
                        load(c + 1, j, NG * c + NG + j)

                group(0)
                sp.wait_ge(neg_done, (2 * c + p) * SP_ + 2)
                if p == 0:
                    load_rows(c, 1, 1)
                else:
                    load_rows(c + 1, 0, 0)
                with sp.Fori(1, HALF) as j:
                    group(j)

            with sp.Fori(0, NC - 1) as c:
                one_pass(c, 0)
                one_pass(c, 1)
            one_pass(NC - 1, 0)

        @block.gpsimd
        def _(pool):
            nc.gpsimd.memset(ident[:, :], 0.0).then_inc(ident_set, 1)
            pool.wait_ge(ident_set, 1)
            nc.gpsimd.affine_select(out=ident[:, :], in_=ident[:, :], compare_op=ALU.not_equal, fill=1.0,
                                    base=0, pattern=[[-1, P]], channel_multiplier=1).then_inc(ident_set, 1)
            nc.gpsimd.memset(half[:, :], -0.5).then_inc(ident_set, 1)
            pool.wait_ge(mx_done, 1)
            nc.gpsimd.partition_all_reduce(M[:, :], mx[:, :], P, RMAX).then_inc(M_done, 1)

            def convert(k):
                for t in range(B):
                    pool.wait_ge(raw_in[t], 16 * k + 16)
                    if t == 0:
                        pool.wait_ge(tp_done, k)
                    pool.sem_inc(pool_passed, 1)
                    nc.gpsimd.tensor_scalar(nat[:, t, :], raw[:, t, :], 0.0, 15.0, ALU.is_gt, ALU.add).then_inc(conv_done, 1)

            with pool.Fori(0, NG // 2) as i:
                convert(i)
                for n in range(2):
                    g = 2 * i + n
                    pool.wait_ge(scaled, 2)
                    pool.wait_ge(lo_done, g)
                    nc.gpsimd.tensor_tensor(
                        out=U2[n].rearrange("p (b h) v -> p b h v", b=B)[:, :, :, 0:O], in0=xt_of(g), in1=e_of(e2, g), op=ALU.mult).then_inc(U2_done, 1)
                    nc.gpsimd.tensor_copy(U2[n][:, :, O], e_flat(e2, g)).then_inc(U2_done, 1)

            def seg_a(c, p, last_p):
                for h in range(HP):
                    n = 2 * last_p + h
                    pool.wait_ge(u_done, n + 3)
                    w = ab[:, bass.ds(c * B, B), HP * p + h, :]
                    nc.gpsimd.tensor_tensor(out=u[:, h], in0=u[:, h], in1=w.unsqueeze(3).broadcast_to([P, B, 2, VO]),
                                            op=ALU.mult).then_inc(wu_done, 1)
                    pool.wait_ge(wu_done, n + 1)
                    nc.gpsimd.tensor_tensor(out=u[:, h, :, 0, :], in0=u[:, h, :, 0, :], in1=u[:, h, :, 1, :],
                                            op=ALU.add).then_inc(t_done, 1)

            def seg_b(c, p, last_p):
                pool.wait_ge(res_in, 16 * c + 16)
                for h in range(HP):
                    n = 2 * last_p + h
                    pool.wait_ge(rden_done, last_p + 1)
                    nc.gpsimd.tensor_tensor(out=u[:, h, :, 1, 0:O], in0=u[:, h, :, 0, 0:O],
                                            in1=rden[:, h, :].unsqueeze(2).broadcast_to([P, B, O]),
                                            op=ALU.mult).then_inc(tr_done, 1)
                    pool.wait_ge(tr_done, n + 1)
                    yh = y[:, :, (HP * p + h) * O:(HP * p + h + 1) * O]
                    nc.gpsimd.tensor_tensor(out=yh, in0=yh, in1=u[:, h, :, 1, 0:O], op=ALU.add).then_inc(y_done, 1)

            def seg_c(c):
                pool.wait_ge(mv_done, c + 1)
                pool.sem_inc(pool_passed, 1)
                nc.gpsimd.tensor_scalar(rstd[:, :], mv[:, :, 1], EPS, None, ALU.add).then_inc(pow_done, 1)
                pool.wait_ge(pow_done, 2 * c + 1)
                nc.gpsimd.tensor_tensor(out=rstd[:, :], in0=rstd[:, :], in1=half[:, :], op=ALU.pow).then_inc(pow_done, 1)
                pool.wait_ge(pow_done, 2 * c + 2)
                pool.sem_inc(pool_passed, 1)
                for t in range(B):
                    nc.gpsimd.tensor_scalar(y[:, t, :], y[:, t, :], mv[:, t, 0:1], rstd[:, t:t + 1],
                                            ALU.subtract, ALU.mult).then_inc(norm_done, 1)
                pool.wait_ge(norm_done, B * c + B)
                pool.dma_start(out_v[c], y[:, :, :]).then_inc(out_done, 16)

            def load_res(c):
                pool.dma_start(y[:, :, :], x_v[c]).then_inc(res_in, 16)

            def one_pass(c, p, first=False, second=False, more=True):
                base = NG * c + (HALF if p == 0 else NG)
                if more:
                    convert(base)
                if not first:
                    seg_a(c - 1 if p == 0 else c, 1 - p, 2 * c + p - 1)
                    if p == 1 and not second:
                        seg_c(c - 1)
                if more:
                    with pool.Fori(1, 3) as j:
                        convert(base + j)
                if not first:
                    if p == 1:
                        if not second:
                            pool.wait_ge(out_done, 16 * c)
                        load_res(c)
                    seg_b(c - 1 if p == 0 else c, 1 - p, 2 * c + p - 1)
                if more:
                    with pool.Fori(3, HALF) as j:
                        convert(base + j)

            one_pass(0, 0, first=True)
            one_pass(0, 1, second=True)
            with pool.Fori(1, NC - 1) as c:
                one_pass(c, 0)
                one_pass(c, 1)
            one_pass(NC - 1, 0)
            one_pass(NC - 1, 1, more=False)
            seg_a(NC - 1, 1, NP - 1)
            seg_b(NC - 1, 1, NP - 1)
            seg_c(NC - 1)
            pool.wait_ge(out_done, 16 * NC)

        @block.scalar
        def _(act):
            with act.Fori(0, NG // 2) as i:
                for n in range(2):
                    g = 2 * i + n
                    act.wait_ge(xTp_done, g + 3)
                    act.wait_ge(xt_done, g + 1)
                    nc.scalar.activation(xT[n].rearrange("p k b q -> p (k b q)"),
                                         acc[:, 0:2, :].rearrange("p k n -> p (k n)"), ACT.Copy).then_inc(xT_done, 1)
            act.wait_ge(sTp_done, 1)
            act.wait_ge(wx_done, 2)
            nc.scalar.activation(sT.rearrange("r h p -> r (h p)"), spare[0:R, 0:H * P], ACT.Copy).then_inc(sT_done, 1)
            act.wait_ge(sT_done, 1)
            act.dma_start(s_dram.rearrange("h (r p) -> r h p", p=P), sT).then_inc(s_out, 16)
            act.wait_ge(exp_in, 4)
            nc.scalar.activation(e1, dM, ACT.Exp).then_inc(exp_done, 1)
            nc.scalar.activation(e2, dM, ACT.Exp, scale=SLOPE).then_inc(exp_done, 1)
            nc.scalar.activation(ab[:, :, :, 0], tN, ACT.Exp).then_inc(exp_done, 1)
            nc.scalar.activation(ab[:, :, :, 1], tP, ACT.Exp).then_inc(exp_done, 1)
            with act.Fori(0, NG // 2) as i:
                for n in range(2):
                    g = 2 * i + n
                    act.wait_ge(U1_done, 2 * g + 2)
                    act.wait_ge(U2_done, 2 * g + 2)
                    nc.scalar.activation(V_part(g, 0), U1[n], ACT.Copy, scale=1.0 / LOW).then_inc(hi_done, 1)
                    nc.scalar.activation(V_part(g, 2), U2[n], ACT.Copy, scale=1.0 / LOW).then_inc(hi_done, 1)

            act.wait_ge(lo_done, NG)

            def signs(P_, g, h, q):
                n = P_ * SP_ + 2 * g + h
                act.wait_ge(neg_done, n + 1)
                for b in range(B - 1):
                    r = (g * B + b) * 2 * H + H + q * HP + h
                    ins = nc.scalar.activation(sgn[:, h, :, b], srow[:, q, h, :], ACT.Sign,
                                               bias=tabf[:, bass.ds(r, 1)], scale=1.0)
                ins.then_inc(sgn_done, 1)

            def low(P_, h):
                act.wait_ge(sums_done, (P_ + 1) * SP_ + h + 1)
                act.wait_ge(y_done, 2 * P_ + h + 1)
                k0, k1 = (u[:, h].rearrange("p t c v -> p (t c) v")[:, 0:6, :], u[:, h].rearrange("p t c v -> p (t c) v")[:, 6:8, :])
                nc.scalar.activation(k0.rearrange("p (k s) v -> p k s v", k=2), acc_part(h, 0, 1), ACT.Copy, scale=1.0 / LOW)
                nc.scalar.activation(k1, acc_part(h, 1, 1), ACT.Copy, scale=1.0 / LOW).then_inc(low_done, 1)

            def one_pass(P_, c, q, first=False):
                act.wait_ge(row_in[q][0], 16 * c + 16)
                act.wait_ge(row_in[q][1], 16 * c + 16)
                signs(P_, 0, 0, q)
                signs(P_, 0, 1, q)
                if not first:
                    low(P_ - 1, 0)
                    low(P_ - 1, 1)
                with act.Fori(1, NG) as g:
                    signs(P_, g, 0, q)
                    signs(P_, g, 1, q)

            one_pass(0, 0, 0, first=True)
            one_pass(1, 0, 1)
            with act.Fori(1, NC) as c:
                one_pass(2 * c, c, 0)
                one_pass(2 * c + 1, c, 1)
            low(NP - 1, 0)
            low(NP - 1, 1)

        @block.vector
        def _(dve):
            dve.sem_inc(xTp_done, 2)
            dve.sem_inc(xt_done, 2)
            dve.sem_inc(conv_done, 4)
            dve.sem_inc(neg_done, 2)
            dve.sem_inc(sums_done, 2)
            dve.sem_inc(u_done, 2)
            dve.sem_inc(y_done, 2)
            dve.wait_ge(w_in, 16 * KF)
            dve.wait_ge(a_in, 16)
            wv = Wx[:, :, 0:F].rearrange("p k (h o) -> p k h o", h=H)
            for n in range(2):
                for k in range(KF):
                    if n and k == 0:
                        dve.wait_ge(wx_done, 1)
                    nc.vector.tensor_tensor(out=prod[:, k], in0=wv[:, k], in1=aB[:, :, n * O:(n + 1) * O],
                                            op=ALU.mult).then_inc(prod_done, 1)
                dve.wait_ge(prod_done, KF * (n + 1))
                nc.vector.tensor_reduce(Wx[:, :, F + n * H:F + (n + 1) * H], prod, AX.X, ALU.add).then_inc(wx_done, 1)
            with dve.Fori(0, NG) as g:
                dve.wait_ge(xt_done, g + 3)
                nc.vector.tensor_copy(
                    V32[:, bass.ds(g * (B * VX), B * VX)].rearrange("p (b n) -> p b n", b=B)[:, :, 0:F],
                    acc[:, 2:2 + B, 0:F])
                nc.vector.tensor_copy(tab[:, bass.ds(g * B, B), :], acc[:, 2:2 + B, F:WX]).then_inc(xt_kept, 1)
            dve.wait_ge(xt_kept, NG)
            nc.vector.tensor_reduce(mx[:, :], tab[:, :, H:2 * H].rearrange("p r h -> p h r"), AX.X, ALU.max).then_inc(mx_done, 1)
            dve.wait_ge(M_done, 1)
            Mb = M[:, :].unsqueeze(1).broadcast_to([P, R, H])
            nc.vector.tensor_tensor(out=dM, in0=tab[:, :, H:2 * H], in1=Mb, op=ALU.subtract).then_inc(exp_in, 1)
            nc.vector.tensor_tensor(out=tM, in0=tab[:, :, 0:H], in1=Mb, op=ALU.add).then_inc(exp_in, 1)
            dve.wait_ge(exp_in, 2)
            nc.vector.tensor_scalar(tN, tM, 1.0 - SLOPE, 0.0, ALU.mult, ALU.min).then_inc(exp_in, 1)
            nc.vector.tensor_scalar(tP, tM, SLOPE - 1.0, 0.0, ALU.mult, ALU.min).then_inc(exp_in, 1)
            dve.wait_ge(sTp_done, 1)
            nc.vector.tensor_scalar(tab[:, :, 0:H], tab[:, :, H:2 * H], -1.0, None, ALU.mult).then_inc(negd_done, 1)
            dve.wait_ge(exp_done, 4)
            nc.vector.tensor_scalar(e1, e1, LOW, None, ALU.mult).then_inc(scaled, 1)
            nc.vector.tensor_scalar(e2, e2, LOW, None, ALU.mult).then_inc(scaled, 1)
            dve.wait_ge(scaled, 2)

            def table1(g, n):
                nc.vector.tensor_tensor(out=U1[n].rearrange("p (b h) v -> p b h v", b=B)[:, :, :, 0:O],
                                        in0=xt_of(g), in1=e_of(e1, g), op=ALU.mult).then_inc(U1_done, 1)
                nc.vector.tensor_copy(U1[n][:, :, O], e_flat(e1, g)).then_inc(U1_done, 1)

            def lows(g, n):
                dve.wait_ge(hi_done, 2 * g + 2)
                nc.vector.scalar_tensor_tensor(out=V_part(g, 1), in0=V_part(g, 0), scalar=-LOW, in1=U1[n],
                                               op0=ALU.mult, op1=ALU.add)
                nc.vector.scalar_tensor_tensor(out=V_part(g, 3), in0=V_part(g, 2), scalar=-LOW, in1=U2[n],
                                               op0=ALU.mult, op1=ALU.add).then_inc(lo_done, 1)

            def keep(g, k):
                dve.wait_ge(tp_done, k + 1)
                nc.vector.tensor_scalar(AT[:, bass.ds(g * CW, CW)], tp[:, :].bitcast(u32), 0x10101010, 2,
                                        ALU.bitwise_and, ALU.logical_shift_left).then_inc(at_done, 1)

            table1(0, 0)
            with dve.Fori(0, HALF - 1) as i:
                table1(2 * i + 1, 1)
                lows(2 * i, 0)
                dve.wait_ge(lo_done, 2 * i + 1)
                table1(2 * i + 2, 0)
                keep(i, i)
                lows(2 * i + 1, 1)
                dve.wait_ge(lo_done, 2 * i + 2)
            table1(NG - 1, 1)
            lows(NG - 2, 0)
            keep(HALF - 1, HALF - 1)
            lows(NG - 1, 1)
            dve.wait_ge(lo_done, NG)
            dve.wait_ge(s_out, 16)
            dve.wait_ge(negd_done, 1)

            def fourth(P_, g, h, q):
                n = P_ * SP_ + 2 * g + h
                r = (g * B + B - 1) * 2 * H + q * HP + h
                dve.wait_ge(neg_done, n + 1)
                nc.vector.tensor_scalar(sgn[:, h, :, B - 1], srow[:, q, h, :], tabf[:, bass.ds(r, 1)], 1.0,
                                        ALU.is_ge, ALU.subtract).then_inc(third_done, 1)

            def masks_of(P_, g, h, q):
                n = P_ * SP_ + 2 * g + h
                at = AT[:, bass.ds(g * CW, CW)]
                dve.wait_ge(at_done, (P_ * HALF if q == 0 else (P_ - 1) * HALF) + g + 1)
                dve.wait_ge(third_done, n + 1)
                dve.wait_ge(sgn_done, n + 1)
                dve.wait_ge(sums_done, n + 1)
                nc.vector.scalar_tensor_tensor(out=word(neg, h), in0=word(sgn, h), scalar=1, in1=at,
                                               op0=ALU.logical_shift_right, op1=ALU.bitwise_and).then_inc(neg_done, 1)

            def rest_of(P_, g, h):
                n = P_ * SP_ + 2 * g + h
                dve.wait_ge(neg_done, n + 3)
                nc.vector.tensor_tensor(out=word(pos, h), in0=AT[:, bass.ds(g * CW, CW)], in1=word(neg, h),
                                        op=ALU.bitwise_xor).then_inc(pos_done, 1)

            def high(P_, h):
                dve.wait_ge(low_done, 2 * P_ + h + 1)
                uv = u[:, h].rearrange("p t c v -> p (t c) v")
                k0 = uv[:, 0:6, :].rearrange("p (k s) v -> p k s v", k=2)
                nc.vector.tensor_tensor(out=k0, in0=k0, in1=acc_part(h, 0, 0), op=ALU.add)
                nc.vector.tensor_tensor(out=uv[:, 6:8, :], in0=uv[:, 6:8, :], in1=acc_part(h, 1, 0),
                                        op=ALU.add).then_inc(u_done, 1)

            def group(P_, g, q, after0=None, after1=None):
                fourth(P_, g, 0, q)
                masks_of(P_, g, 0, q)
                fourth(P_, g, 1, q)
                rest_of(P_, g, 0)
                if after0:
                    after0()
                masks_of(P_, g, 1, q)
                rest_of(P_, g, 1)
                if after1:
                    after1()

            def two_groups(P_, c, j, q, more, last=None):
                k = P_ * HALF + HALF + j
                group(P_, 2 * j, q, *((lambda: high(last, 0), lambda: high(last, 1)) if last is not None else ()))
                if more:
                    dve.wait_ge(pos_done, P_ * SP_ + 4 * j + 2)
                    keep(j if q == 1 else j + HALF, k)
                group(P_, 2 * j + 1, q)

            def inverse(last):
                dve.wait_ge(t_done, 2 * last + 2)
                dve.wait_ge(y_done, 2 * last + 2)
                nc.vector.reciprocal(rden[:, :, :], u[:, :, :, 0, O]).then_inc(rden_done, 1)

            def moments(c):
                dve.wait_ge(y_done, 4 * c + 6)
                for t in range(B):
                    nc.vector.bn_stats(stats[:, t, :], y[:, t, :]).then_inc(stats_done, 1)
                dve.wait_ge(stats_done, B * c + B)
                dve.sem_inc(dve_passed, 1)
                for t in range(B):
                    ins = nc.vector.bn_aggr(mv[:, t, :], stats[:, t, :])
                ins.then_inc(mv_done, 1)

            def one_pass(P_, c, q, first=False, more=True, stat=True):
                dve.wait_ge(row_in[q][0], 16 * c + 16)
                dve.wait_ge(row_in[q][1], 16 * c + 16)
                two_groups(P_, c, 0, q, more, None if first else P_ - 1)
                two_groups(P_, c, 1, q, more)
                if not first:
                    inverse(P_ - 1)
                with dve.Fori(2, HALF) as j:
                    two_groups(P_, c, j, q, more)
                if q == 0 and not first:
                    moments(c - 1)

            one_pass(0, 0, 0, first=True)
            one_pass(1, 0, 1)
            with dve.Fori(1, NC - 1) as c:
                one_pass(2 * c, c, 0)
                one_pass(2 * c + 1, c, 1)
            one_pass(NP - 2, NC - 1, 0)
            one_pass(NP - 1, NC - 1, 1, more=False)
            high(NP - 1, 0)
            high(NP - 1, 1)
            inverse(NP - 1)
            moments(NC - 1)

        @block.tensor
        def _(pe):
            pe.wait_ge(ident_set, 3)

            def turn_x(g, n, i):
                pe.wait_ge(x_in[n], 16 * i + 16)
                pe.wait_ge(xT_done, g)
                for k in range(KF):
                    for b in range(B):
                        ins = nc.tensor.transpose(acc[:, k, b * P:(b + 1) * P], xg[n][:, b, k * P:(k + 1) * P], ident[:, :])
                ins.then_inc(xTp_done, 1)

            def project(g, n):
                pe.wait_ge(xT_done, g + 1)
                pe.wait_ge(xt_kept, g)
                for b in range(B):
                    for k in range(KF):
                        ins = nc.tensor.matmul(acc[:, 2 + b, 0:WX], xT[n][:, k, b, :], Wx[:, k, :],
                                               start=(k == 0), stop=(k == KF - 1))
                ins.then_inc(xt_done, 1)

            turn_x(0, 0, 0)
            pe.wait_ge(wx_done, 2)
            with pe.Fori(0, NG // 2 - 1) as i:
                turn_x(2 * i + 1, 1, i)
                project(2 * i, 0)
                turn_x(2 * i + 2, 0, i + 1)
                project(2 * i + 1, 1)
            turn_x(NG - 1, 1, NG // 2 - 1)
            project(NG - 2, 0)
            project(NG - 1, 1)
            pe.wait_ge(xt_kept, NG)
            for h in range(H):
                ins = nc.tensor.transpose(spare[0:R, h * P:(h + 1) * P], tab[:, :, h], ident[:, :])
            ins.then_inc(sTp_done, 1)

            def turn_masks(k):
                pe.wait_ge(conv_done, 4 * k + 8)
                pe.wait_ge(at_done, k)
                for t in range(B):
                    ins = nc.tensor.transpose(tp[:, t * P:(t + 1) * P], nat[:, t, :].bitcast(fp32), ident[:, :])
                ins.then_inc(tp_done, 1)

            with pe.Fori(0, HALF) as k:
                turn_masks(k)

            def sums(P_, g, h, base, first):
                pe.wait_ge(pos_done, P_ * SP_ + 2 * g + h + 1)
                if first:
                    pe.wait_ge(u_done, 2 * P_ + h + 1)
                pe.sem_inc(pe_passed, 1)
                opened = set()
                for b in range(B):
                    for cd, m in ((0, pos), (1, neg)):
                        for t in range(B):
                            k, o = slot(t, cd)
                            opens = first and k not in opened
                            opened.add(k)
                            v = base + b * VW + h * HV + cd * 2 * VO
                            ins = nc.tensor.matmul(acc[:, 3 * h + k, o:o + 2 * VO], m[:, h, t * P:(t + 1) * P, b],
                                                   V[:, v:v + 2 * VO],
                                                   start=opens,
                                                   stop=False, skip_group_check=True)
                ins.then_inc(sums_done, 1)

            def one_pass(c, p, more):
                P_ = 2 * c + p
                for j in range(HALF):
                    if more:
                        turn_masks(P_ * HALF + HALF + j)
                    for g in (2 * j, 2 * j + 1):
                        for h in range(HP):
                            sums(P_, g, h, g * (B * VW) + p * (HP * HV), g == 0)

            with pe.Fori(0, NC - 1) as c:
                one_pass(c, 0, True)
                one_pass(c, 1, True)
            one_pass(NC - 1, 0, True)
            one_pass(NC - 1, 1, False)


_INS = ['x', 'adj', 'L0_gnn_W', 'L0_gnn_a']
_OUTS = [((8192, 256), 'float32')]


def kernel(**inputs):
    import numpy as _np
    import concourse.bacc as _bacc
    from concourse import mybir as _mybir
    from concourse.bass_utils import run_bass_kernel_spmd as _run

    nc = _bacc.Bacc("TRN2", target_bir_lowering=False, num_devices=1)
    arrays, args = {}, []
    for name in _INS:
        a = _np.ascontiguousarray(inputs[name])
        arrays[f"in_{name}_dram"] = a
        args.append(nc.dram_tensor(f"in_{name}_dram", a.shape, _mybir.dt.from_np(a.dtype), kind="ExternalInput").ap())
    for i, (shape, dtype) in enumerate(_OUTS):
        dt = _mybir.dt.from_np(_np.dtype(dtype))
        args.append(nc.dram_tensor(f"out_{i}_dram", shape, dt, kind="ExternalOutput").ap())
    gat_residual_norm(nc, *args)
    r = _run(nc, [arrays], core_ids=[0])
    return r.results[0]["out_0_dram"]
```

```python
import concourse.bass as bass
from concourse import mybir
from contextlib import ExitStack



def gat_residual_norm(nc: bass.Bass, x: bass.AP, adj: bass.AP, W: bass.AP, a: bass.AP, out: bass.AP):
    fp32 = mybir.dt.float32
    fp16 = mybir.dt.float16
    fp8 = mybir.dt.float8e4
    u32 = mybir.dt.uint32
    i32 = mybir.dt.int32
    i8 = mybir.dt.int8
    u8 = mybir.dt.uint8
    ALU = mybir.AluOpType
    ACT = mybir.ActivationFunctionType
    AX = mybir.AxisListType
    RMAX = bass.bass_isa.ReduceOp.max

    P = 128
    N, F = x.shape
    H, _, O = W.shape
    B = 4
    CW = B * P
    NC = N // CW
    NG = N // CW
    R = N // P
    KF = F // P
    VO = O + 1
    HV = 4 * VO
    VW = H * HV
    VX = VW // 2
    HP = 2
    NP = NC * (H // HP)
    WX = F + 2 * H
    SLOPE = 0.2
    EPS = 1e-5
    LOW = 2.0 ** 14
    QUEUE = 4 * HP * B
    assert N % CW == 0 and F == KF * P and H == 4 and H * O == F and QUEUE == 32
    HALF = NG // 2
    SP_ = 2 * NG

    ctx = ExitStack()
    with ctx:
        def sb(name, shape, dt):
            return ctx.enter_context(nc.sbuf_tensor(name, shape, dt))

        def sem(name):
            return ctx.enter_context(nc.semaphore(name))

        V = sb("V", [P, R * VW], fp16)
        V32 = V[:, :].bitcast(fp32)
        AT = sb("AT", [P, NG * CW], u32)
        raw = sb("raw", [P, B, CW], i32)
        nat = sb("nat", [P, B, CW], u8)
        srow = sb("srow", [P, 2, HP, CW], fp32)
        sgn = sb("sgn", [P, HP, CW, B], i8)
        pos = sb("pos", [P, HP, CW, B], fp8)
        neg = sb("neg", [P, HP, CW, B], fp8)
        u = sb("u", [P, HP, B, 2, VO], fp32)
        y = sb("y", [P, B, F], fp32)
        tab = sb("tab", [P, R, 2 * H], fp32)
        ab = sb("ab", [P, R, H, 2], fp32)
        ident = sb("ident", [P, P], fp32)
        mx = sb("mx", [P, H], fp32)
        M = sb("M", [P, H], fp32)
        rden = sb("rden", [P, HP, B], fp32)
        stats = sb("stats", [P, B, 6], fp32)
        mv = sb("mv", [P, B, 2], fp32)
        rstd = sb("rstd", [P, B], fp32)
        half = sb("half", [P, B], fp32)

        late = AT[:, HALF * CW:NG * CW].bitcast(fp32)
        xg = [late[:, n * B * F:(n + 1) * B * F].rearrange("p (b f) -> p b f", b=B) for n in range(2)]
        xT = [late[:, (2 + n) * B * F:(3 + n) * B * F].rearrange("p (k b q) -> p k b q", k=KF, b=B) for n in range(2)]
        UW = B * H * VO
        U1 = [late[:, n * UW:(n + 1) * UW].rearrange("p (r v) -> p r v", v=VO) for n in range(2)]
        masks = [m[:, :, :, :].rearrange("p h i b -> p (h i b)").bitcast(fp32) for m in (sgn, pos, neg)]
        Wx = y[:, :, :].rearrange("p b f -> p (b f)")[:, 0:KF * WX].rearrange("p (k n) -> p k n", k=KF)
        aB = masks[0][:, 0:H * 2 * O].rearrange("p (h n) -> p h n", h=H)
        prod = masks[1][:, 0:KF * F].rearrange("p (k h o) -> p k h o", k=KF, h=H)
        dM = masks[2][:, 0:R * H].rearrange("p (r h) -> p r h", h=H)
        tM = masks[2][:, R * H:2 * R * H].rearrange("p (r h) -> p r h", h=H)
        tN = masks[2][:, 2 * R * H:3 * R * H].rearrange("p (r h) -> p r h", h=H)
        tP = masks[2][:, 3 * R * H:4 * R * H].rearrange("p (r h) -> p r h", h=H)
        e1 = masks[0][:, 0:R * H].rearrange("p (r h) -> p r h", h=H)
        e2 = masks[0][:, R * H:2 * R * H].rearrange("p (r h) -> p r h", h=H)
        uall = u[:, :, :, :, :].rearrange("p h b c v -> p (h b c v)")
        U2 = [uall.rearrange("p (r v) -> p r v", v=VO), late[:, 2 * UW:3 * UW].rearrange("p (r v) -> p r v", v=VO)]
        sT = masks[1][0:R, 0:H * P].rearrange("r (h p) -> r h p", h=H)

        acc = ctx.enter_context(nc.psum_tensor("acc", [P, 6, 512], fp32))
        tp = ctx.enter_context(nc.psum_tensor("tp", [P, 512], fp32))
        spare = ctx.enter_context(nc.psum_tensor("spare", [P, 512], fp32))

        s_dram = nc.dram_tensor("s_rows", [H, N], fp32, kind="Internal").ap()

        w_in = sem("w_in")
        a_in = sem("a_in")
        x_in = [sem("x_in0"), sem("x_in1")]
        ident_set = sem("ident_set")
        prod_done = sem("prod_done")
        wx_done = sem("wx_done")
        xTp_done = sem("xTp_done")
        xT_done = sem("xT_done")
        xt_done = sem("xt_done")
        xt_kept = sem("xt_kept")
        mx_done = sem("mx_done")
        M_done = sem("M_done")
        exp_in = sem("exp_in")
        exp_done = sem("exp_done")
        scaled = sem("scaled")
        sTp_done = sem("sTp_done")
        sT_done = sem("sT_done")
        s_out = sem("s_out")
        negd_done = sem("negd_done")
        U1_done = sem("U1_done")
        U2_done = sem("U2_done")
        hi_done = sem("hi_done")
        lo_done = sem("lo_done")
        raw_in = [sem(f"raw_in{t}") for t in range(B)]
        conv_done = sem("conv_done")
        tp_done = sem("tp_done")
        at_done = sem("at_done")
        row_in = [[sem(f"row_in{q}{h}") for h in range(HP)] for q in range(2)]
        fourth_done = sem("fourth_done")
        sgn_done = sem("sgn_done")
        neg_done = sem("neg_done")
        pos_done = sem("pos_done")
        sums_done = sem("sums_done")
        low_done = sem("low_done")
        u_done = sem("u_done")
        wu_done = sem("wu_done")
        t_done = sem("t_done")
        rden_done = sem("rden_done")
        tr_done = sem("tr_done")
        y_done = sem("y_done")
        res_in = sem("res_in")
        stats_done = sem("stats_done")
        mv_done = sem("mv_done")
        pow_done = sem("pow_done")
        norm_done = sem("norm_done")
        out_done = sem("out_done")
        pe_passed = sem("pe_passed")
        pool_passed = sem("pool_passed")
        dve_passed = sem("dve_passed")

        block = ctx.enter_context(nc.Block())

        adj_v = adj.rearrange("(c p t) (g w) -> c g p t w", p=P, t=B, w=CW)
        x_v = x.rearrange("(g p b) f -> g p b f", p=P, b=B)
        out_v = out.rearrange("(g p b) f -> g p b f", p=P, b=B)
        s_v = s_dram.rearrange("h (c w) -> h c w", w=CW)

        sgn8 = sgn[:, :, :, :].bitcast(mybir.dt.float8e5)

        def word(t, h):
            return t[:, h, :, :].rearrange("p i b -> p (i b)").bitcast(u32)

        def slot(t, cd):
            q = t * 2 + cd
            return q // 3, (q % 3) * 2 * VO

        def xt_of(g):
            return V32[:, bass.ds(g * (B * VX), B * VX)].rearrange("p (b n) -> p b n", b=B)[:, :, 0:F] \
                .rearrange("p b (h o) -> p b h o", h=H)

        def e_of(e, g):
            return e[:, bass.ds(g * B, B), :].unsqueeze(3).broadcast_to([P, B, H, O])

        def e_flat(e, g):
            return e[:, bass.ds(g * B, B), :].rearrange("p b h -> p (b h)")

        def V_part(g, part):
            return V[:, bass.ds(g * (B * VW), B * VW)].rearrange("p (r n) -> p r n", n=HV)[:, :, part * VO:(part + 1) * VO]

        tabf = tab[:, :, :].rearrange("p r n -> p (r n)")

        def acc_part(h, rect, part):
            if rect == 0:
                v = acc[:, 3 * h:3 * h + 2, 0:3 * 2 * VO].rearrange("p k (s n) -> p k s n", s=3)
                return v[:, :, :, part * VO:(part + 1) * VO]
            v = acc[:, 3 * h + 2, 0:2 * 2 * VO].rearrange("p (s n) -> p s n", s=2)
            return v[:, :, part * VO:(part + 1) * VO]


        @block.sync
        def _(sp):
            for k in range(KF):
                sp.dma_start(Wx[:, k, 0:F].rearrange("p (h o) -> p h o", h=H),
                             W[:, k * P:(k + 1) * P, :].rearrange("h p o -> p h o")).then_inc(w_in, 16)
            sp.dma_start(aB, a.rearrange("(q h) n -> q h n", q=1).broadcast_to([P, H, 2 * O])).then_inc(a_in, 16)
            with sp.Fori(0, NG // 2) as i:
                for n in range(2):
                    sp.wait_ge(xTp_done, 2 * i + n + 1)
                    sp.dma_start(xg[n], x_v[2 * i + n]).then_inc(x_in[n], 16)

            def load(c, g, k):
                for t in range(B):
                    sp.wait_ge(conv_done, 4 * k + t + 1)
                    sp.dma_start(raw[:, t, :], adj_v[c, g, :, t, :]).then_inc(raw_in[t], 16)

            def load_rows(c, p, q):
                for h in range(HP):
                    sp.dma_start(srow[:, q, h, :], s_v[HP * p + h, c].partition_broadcast(P)).then_inc(row_in[q][h], 16)

            with sp.Fori(0, HALF) as g:
                load(0, g, g)
            sp.wait_ge(s_out, 16)
            sp.wait_ge(lo_done, NG)
            load_rows(0, 0, 0)

            def one_pass(c, p):
                def group(j):
                    if p == 0:
                        load(c, HALF + j, NG * c + HALF + j)
                    else:
                        load(c + 1, j, NG * c + NG + j)

                group(0)
                sp.wait_ge(neg_done, (2 * c + p) * SP_ + 2)
                if p == 0:
                    load_rows(c, 1, 1)
                else:
                    load_rows(c + 1, 0, 0)
                with sp.Fori(1, HALF) as j:
                    group(j)

            with sp.Fori(0, NC - 1) as c:
                one_pass(c, 0)
                one_pass(c, 1)
            one_pass(NC - 1, 0)

        @block.gpsimd
        def _(pool):
            nc.gpsimd.memset(ident[:, :], 0.0).then_inc(ident_set, 1)
            pool.wait_ge(ident_set, 1)
            nc.gpsimd.affine_select(out=ident[:, :], in_=ident[:, :], compare_op=ALU.not_equal, fill=1.0,
                                    base=0, pattern=[[-1, P]], channel_multiplier=1).then_inc(ident_set, 1)
            nc.gpsimd.memset(half[:, :], -0.5).then_inc(ident_set, 1)
            pool.wait_ge(mx_done, 1)
            nc.gpsimd.partition_all_reduce(M[:, :], mx[:, :], P, RMAX).then_inc(M_done, 1)

            with pool.Fori(0, NG // 2) as i:
                for n in range(2):
                    g = 2 * i + n
                    pool.wait_ge(scaled, 2)
                    pool.wait_ge(lo_done, g)
                    nc.gpsimd.tensor_tensor(
                        out=U2[n].rearrange("p (b h) v -> p b h v", b=B)[:, :, :, 0:O], in0=xt_of(g), in1=e_of(e2, g), op=ALU.mult).then_inc(U2_done, 1)
                    nc.gpsimd.tensor_copy(U2[n][:, :, O], e_flat(e2, g)).then_inc(U2_done, 1)

            pool.wait_ge(lo_done, NG)

            def fourth(P_, g, h, p):
                n = P_ * SP_ + 2 * g + h
                pool.wait_ge(neg_done, n + 1)
                pool.sem_inc(pool_passed, 1)
                r = (g * B + B - 1) * 2 * H + HP * p + h
                nc.gpsimd.tensor_tensor(out=sgn8[:, h, :, B - 1], in0=srow[:, p, h, :],
                                        in1=tabf[:, r:r + 1].broadcast_to([P, CW]), op=ALU.subtract,
                                        saturate=False).then_inc(fourth_done, 1)

            def weigh(c, p, last, h):
                pool.wait_ge(u_done, 2 * last + h + 3)
                w = ab[:, bass.ds(c * B, B), HP * p + h, :]
                nc.gpsimd.tensor_tensor(out=u[:, h], in0=u[:, h], in1=w.unsqueeze(3).broadcast_to([P, B, 2, VO]),
                                        op=ALU.mult).then_inc(wu_done, 1)

            def join(last, h):
                pool.wait_ge(wu_done, 2 * last + h + 1)
                nc.gpsimd.tensor_tensor(out=u[:, h, :, 0, :], in0=u[:, h, :, 0, :], in1=u[:, h, :, 1, :],
                                        op=ALU.add).then_inc(t_done, 1)

            def divide(last, h):
                pool.wait_ge(rden_done, last + 1)
                nc.gpsimd.tensor_tensor(out=u[:, h, :, 1, 0:O], in0=u[:, h, :, 0, 0:O],
                                        in1=rden[:, h, :].unsqueeze(2).broadcast_to([P, B, O]),
                                        op=ALU.mult).then_inc(tr_done, 1)

            def add_on(c, p, last, h):
                pool.wait_ge(res_in, 16 * c + 16)
                pool.wait_ge(tr_done, 2 * last + h + 1)
                yh = y[:, :, (HP * p + h) * O:(HP * p + h + 1) * O]
                nc.gpsimd.tensor_tensor(out=yh, in0=yh, in1=u[:, h, :, 1, 0:O], op=ALU.add).then_inc(y_done, 1)

            def deviation(c):
                pool.wait_ge(mv_done, c + 1)
                pool.sem_inc(pool_passed, 1)
                nc.gpsimd.tensor_scalar(rstd[:, :], mv[:, :, 1], EPS, None, ALU.add).then_inc(pow_done, 1)
                pool.wait_ge(pow_done, 2 * c + 1)
                nc.gpsimd.tensor_tensor(out=rstd[:, :], in0=rstd[:, :], in1=half[:, :], op=ALU.pow).then_inc(pow_done, 1)

            def normalise(c, t):
                pool.wait_ge(pow_done, 2 * c + 2)
                pool.sem_inc(pool_passed, 1)
                nc.gpsimd.tensor_scalar(y[:, t, :], y[:, t, :], mv[:, t, 0:1], rstd[:, t:t + 1],
                                        ALU.subtract, ALU.mult).then_inc(norm_done, 1)

            def store(c):
                pool.wait_ge(norm_done, B * c + B)
                pool.dma_start(out_v[c], y[:, :, :]).then_inc(out_done, 16)

            def load_res(c):
                pool.dma_start(y[:, :, :], x_v[c]).then_inc(res_in, 16)

            def one_pass(c, p, first=False, second=False):
                P_ = 2 * c + p
                ec, ep, last = (c - 1, 1, P_ - 1) if p == 0 else (c, 0, P_ - 1)
                pool.wait_ge(row_in[p][0], 16 * c + 16)
                pool.wait_ge(row_in[p][1], 16 * c + 16)
                for g in range(NG):
                    for h in range(HP):
                        fourth(P_, g, h, p)
                    if p == 1 and not second:
                        if g == 0:
                            deviation(c - 1)
                        if 1 <= g <= B:
                            normalise(c - 1, g - 1)
                        if g == B:
                            store(c - 1)
                    if p == 1 and g == 8:
                        if not second:
                            pool.wait_ge(out_done, 16 * c)
                        load_res(c)
                    if not first:
                        if g in (5, 7):
                            weigh(ec, ep, last, (g - 5) // 2)
                        if g in (6, 8):
                            join(last, (g - 6) // 2)
                        if g in (11, 13):
                            divide(last, (g - 11) // 2)
                        if g in (12, 14):
                            add_on(ec, ep, last, (g - 12) // 2)

            one_pass(0, 0, first=True)
            one_pass(0, 1, second=True)
            with pool.Fori(1, NC) as c:
                one_pass(c, 0)
                one_pass(c, 1)
            for h in range(HP):
                weigh(NC - 1, 1, NP - 1, h)
                join(NP - 1, h)
            for h in range(HP):
                divide(NP - 1, h)
                add_on(NC - 1, 1, NP - 1, h)
            deviation(NC - 1)
            for t in range(B):
                normalise(NC - 1, t)
            store(NC - 1)
            pool.wait_ge(out_done, 16 * NC)

        @block.scalar
        def _(act):
            with act.Fori(0, NG // 2) as i:
                for n in range(2):
                    g = 2 * i + n
                    act.wait_ge(xTp_done, g + 3)
                    act.wait_ge(xt_done, g + 1)
                    nc.scalar.activation(xT[n].rearrange("p k b q -> p (k b q)"),
                                         acc[:, 0:2, :].rearrange("p k n -> p (k n)"), ACT.Copy).then_inc(xT_done, 1)
            act.wait_ge(sTp_done, 1)
            act.wait_ge(wx_done, 2)
            nc.scalar.activation(sT.rearrange("r h p -> r (h p)"), spare[0:R, 0:H * P], ACT.Copy).then_inc(sT_done, 1)
            act.wait_ge(sT_done, 1)
            act.dma_start(s_dram.rearrange("h (r p) -> r h p", p=P), sT).then_inc(s_out, 16)
            act.wait_ge(exp_in, 4)
            nc.scalar.activation(e1, dM, ACT.Exp).then_inc(exp_done, 1)
            nc.scalar.activation(e2, dM, ACT.Exp, scale=SLOPE).then_inc(exp_done, 1)
            nc.scalar.activation(ab[:, :, :, 0], tN, ACT.Exp).then_inc(exp_done, 1)
            nc.scalar.activation(ab[:, :, :, 1], tP, ACT.Exp).then_inc(exp_done, 1)
            with act.Fori(0, NG // 2) as i:
                for n in range(2):
                    g = 2 * i + n
                    act.wait_ge(U1_done, 2 * g + 2)
                    act.wait_ge(U2_done, 2 * g + 2)
                    nc.scalar.activation(V_part(g, 0), U1[n], ACT.Copy, scale=1.0 / LOW).then_inc(hi_done, 1)
                    nc.scalar.activation(V_part(g, 2), U2[n], ACT.Copy, scale=1.0 / LOW).then_inc(hi_done, 1)

            act.wait_ge(lo_done, NG)

            def signs(P_, g, h, q):
                n = P_ * SP_ + 2 * g + h
                act.wait_ge(neg_done, n + 1)
                for b in range(B - 1):
                    r = (g * B + b) * 2 * H + H + q * HP + h
                    ins = nc.scalar.activation(sgn[:, h, :, b], srow[:, q, h, :], ACT.Sign,
                                               bias=tabf[:, bass.ds(r, 1)], scale=1.0)
                ins.then_inc(sgn_done, 1)

            def low(P_, h):
                act.wait_ge(sums_done, (P_ + 1) * SP_ + h + 1)
                act.wait_ge(y_done, 2 * P_ + h + 1)
                k0, k1 = (u[:, h].rearrange("p t c v -> p (t c) v")[:, 0:6, :], u[:, h].rearrange("p t c v -> p (t c) v")[:, 6:8, :])
                nc.scalar.activation(k0.rearrange("p (k s) v -> p k s v", k=2), acc_part(h, 0, 1), ACT.Copy, scale=1.0 / LOW)
                nc.scalar.activation(k1, acc_part(h, 1, 1), ACT.Copy, scale=1.0 / LOW).then_inc(low_done, 1)

            def one_pass(P_, c, q, first=False):
                act.wait_ge(row_in[q][0], 16 * c + 16)
                act.wait_ge(row_in[q][1], 16 * c + 16)
                signs(P_, 0, 0, q)
                signs(P_, 0, 1, q)
                if not first:
                    low(P_ - 1, 0)
                    low(P_ - 1, 1)
                with act.Fori(1, NG) as g:
                    signs(P_, g, 0, q)
                    signs(P_, g, 1, q)

            one_pass(0, 0, 0, first=True)
            one_pass(1, 0, 1)
            with act.Fori(1, NC) as c:
                one_pass(2 * c, c, 0)
                one_pass(2 * c + 1, c, 1)
            low(NP - 1, 0)
            low(NP - 1, 1)

        @block.vector
        def _(dve):
            dve.sem_inc(xTp_done, 2)
            dve.sem_inc(xt_done, 2)
            dve.sem_inc(conv_done, 4)
            dve.sem_inc(neg_done, 2)
            dve.sem_inc(sums_done, 2)
            dve.sem_inc(u_done, 2)
            dve.sem_inc(y_done, 2)
            dve.wait_ge(w_in, 16 * KF)
            dve.wait_ge(a_in, 16)
            wv = Wx[:, :, 0:F].rearrange("p k (h o) -> p k h o", h=H)
            for n in range(2):
                for k in range(KF):
                    if n and k == 0:
                        dve.wait_ge(wx_done, 1)
                    nc.vector.tensor_tensor(out=prod[:, k], in0=wv[:, k], in1=aB[:, :, n * O:(n + 1) * O],
                                            op=ALU.mult).then_inc(prod_done, 1)
                dve.wait_ge(prod_done, KF * (n + 1))
                nc.vector.tensor_reduce(Wx[:, :, F + n * H:F + (n + 1) * H], prod, AX.X, ALU.add).then_inc(wx_done, 1)
            with dve.Fori(0, NG) as g:
                dve.wait_ge(xt_done, g + 3)
                nc.vector.tensor_copy(
                    V32[:, bass.ds(g * (B * VX), B * VX)].rearrange("p (b n) -> p b n", b=B)[:, :, 0:F],
                    acc[:, 2:2 + B, 0:F])
                nc.vector.tensor_copy(tab[:, bass.ds(g * B, B), :], acc[:, 2:2 + B, F:WX]).then_inc(xt_kept, 1)
            dve.wait_ge(xt_kept, NG)
            nc.vector.tensor_reduce(mx[:, :], tab[:, :, H:2 * H].rearrange("p r h -> p h r"), AX.X, ALU.max).then_inc(mx_done, 1)
            dve.wait_ge(M_done, 1)
            Mb = M[:, :].unsqueeze(1).broadcast_to([P, R, H])
            nc.vector.tensor_tensor(out=dM, in0=tab[:, :, H:2 * H], in1=Mb, op=ALU.subtract).then_inc(exp_in, 1)
            nc.vector.tensor_tensor(out=tM, in0=tab[:, :, 0:H], in1=Mb, op=ALU.add).then_inc(exp_in, 1)
            dve.wait_ge(exp_in, 2)
            nc.vector.tensor_scalar(tN, tM, 1.0 - SLOPE, 0.0, ALU.mult, ALU.min).then_inc(exp_in, 1)
            nc.vector.tensor_scalar(tP, tM, SLOPE - 1.0, 0.0, ALU.mult, ALU.min).then_inc(exp_in, 1)
            dve.wait_ge(sTp_done, 1)
            nc.vector.tensor_scalar(tab[:, :, 0:H], tab[:, :, H:2 * H], -1.0, None, ALU.mult).then_inc(negd_done, 1)
            dve.wait_ge(exp_done, 4)
            nc.vector.tensor_scalar(e1, e1, LOW, None, ALU.mult).then_inc(scaled, 1)
            nc.vector.tensor_scalar(e2, e2, LOW, None, ALU.mult).then_inc(scaled, 1)
            dve.wait_ge(scaled, 2)

            def table1(g, n):
                nc.vector.tensor_tensor(out=U1[n].rearrange("p (b h) v -> p b h v", b=B)[:, :, :, 0:O],
                                        in0=xt_of(g), in1=e_of(e1, g), op=ALU.mult).then_inc(U1_done, 1)
                nc.vector.tensor_copy(U1[n][:, :, O], e_flat(e1, g)).then_inc(U1_done, 1)

            def lows(g, n):
                dve.wait_ge(hi_done, 2 * g + 2)
                nc.vector.scalar_tensor_tensor(out=V_part(g, 1), in0=V_part(g, 0), scalar=-LOW, in1=U1[n],
                                               op0=ALU.mult, op1=ALU.add)
                nc.vector.scalar_tensor_tensor(out=V_part(g, 3), in0=V_part(g, 2), scalar=-LOW, in1=U2[n],
                                               op0=ALU.mult, op1=ALU.add).then_inc(lo_done, 1)

            def keep(g, k):
                dve.wait_ge(tp_done, k + 1)
                nc.vector.tensor_scalar(AT[:, bass.ds(g * CW, CW)], tp[:, :].bitcast(u32), 0x10101010, 2,
                                        ALU.bitwise_and, ALU.logical_shift_left).then_inc(at_done, 1)

            def convert(k, ts):
                for t in ts:
                    dve.wait_ge(raw_in[t], 16 * k + 16)
                    dve.wait_ge(tp_done, k)
                    nc.vector.tensor_scalar(nat[:, t, :], raw[:, t, :], 0.0, 15.0, ALU.is_gt, ALU.add).then_inc(conv_done, 1)

            table1(0, 0)
            convert(0, range(B))
            with dve.Fori(0, HALF - 1) as i:
                table1(2 * i + 1, 1)
                lows(2 * i, 0)
                dve.wait_ge(lo_done, 2 * i + 1)
                table1(2 * i + 2, 0)
                keep(i, i)
                convert(i + 1, range(B))
                lows(2 * i + 1, 1)
                dve.wait_ge(lo_done, 2 * i + 2)
            table1(NG - 1, 1)
            lows(NG - 2, 0)
            keep(HALF - 1, HALF - 1)
            lows(NG - 1, 1)
            convert(HALF, range(B))
            dve.wait_ge(lo_done, NG)
            dve.wait_ge(s_out, 16)
            dve.wait_ge(negd_done, 1)

            def masks_of(P_, g, h, q):
                n = P_ * SP_ + 2 * g + h
                at = AT[:, bass.ds(g * CW, CW)]
                dve.wait_ge(at_done, (P_ * HALF if q == 0 else (P_ - 1) * HALF) + g + 1)
                dve.wait_ge(fourth_done, n + 1)
                dve.wait_ge(sgn_done, n + 1)
                dve.wait_ge(sums_done, n + 1)
                nc.vector.scalar_tensor_tensor(out=word(neg, h), in0=word(sgn, h), scalar=1, in1=at,
                                               op0=ALU.logical_shift_right, op1=ALU.bitwise_and).then_inc(neg_done, 1)

            def rest_of(P_, g, h):
                n = P_ * SP_ + 2 * g + h
                dve.wait_ge(neg_done, n + 3)
                nc.vector.tensor_tensor(out=word(pos, h), in0=AT[:, bass.ds(g * CW, CW)], in1=word(neg, h),
                                        op=ALU.bitwise_xor).then_inc(pos_done, 1)

            def high(P_, h):
                dve.wait_ge(low_done, 2 * P_ + h + 1)
                uv = u[:, h].rearrange("p t c v -> p (t c) v")
                k0 = uv[:, 0:6, :].rearrange("p (k s) v -> p k s v", k=2)
                nc.vector.tensor_tensor(out=k0, in0=k0, in1=acc_part(h, 0, 0), op=ALU.add)
                nc.vector.tensor_tensor(out=uv[:, 6:8, :], in0=uv[:, 6:8, :], in1=acc_part(h, 1, 0),
                                        op=ALU.add).then_inc(u_done, 1)

            def two_groups(P_, j, q, more, last=None, ahead=True):
                k = P_ * HALF + HALF + j
                for d in range(2):
                    g = 2 * j + d
                    for h in range(HP):
                        masks_of(P_, g, h, q)
                        rest_of(P_, g, h)
                        if last is not None and d == 0:
                            high(last, h)
                        if more and ahead and d == 1:
                            convert(k + 1, (2 + h,))
                    if more and d == 0:
                        dve.wait_ge(pos_done, P_ * SP_ + 4 * j + 2)
                        keep(j if q == 1 else j + HALF, k)
                        if ahead:
                            convert(k + 1, (0, 1))

            def inverse(last):
                dve.wait_ge(t_done, 2 * last + 2)
                dve.wait_ge(y_done, 2 * last + 2)
                nc.vector.reciprocal(rden[:, :, :], u[:, :, :, 0, O]).then_inc(rden_done, 1)

            def moments(c):
                dve.wait_ge(y_done, 4 * c + 6)
                for t in range(B):
                    nc.vector.bn_stats(stats[:, t, :], y[:, t, :]).then_inc(stats_done, 1)
                dve.wait_ge(stats_done, B * c + B)
                dve.sem_inc(dve_passed, 1)
                for t in range(B):
                    ins = nc.vector.bn_aggr(mv[:, t, :], stats[:, t, :])
                ins.then_inc(mv_done, 1)

            def one_pass(P_, c, q, first=False, more=True, ends=False):
                two_groups(P_, 0, q, more, None if first else P_ - 1)
                with dve.Fori(1, 5) as j:
                    two_groups(P_, j, q, more)
                if not first:
                    inverse(P_ - 1)
                with dve.Fori(5, HALF - 1 if ends else HALF) as j:
                    two_groups(P_, j, q, more)
                if ends:
                    two_groups(P_, HALF - 1, q, more, ahead=False)
                if q == 0 and not first:
                    moments(c - 1)

            one_pass(0, 0, 0, first=True)
            one_pass(1, 0, 1)
            with dve.Fori(1, NC - 1) as c:
                one_pass(2 * c, c, 0)
                one_pass(2 * c + 1, c, 1)
            one_pass(NP - 2, NC - 1, 0, ends=True)
            one_pass(NP - 1, NC - 1, 1, more=False)
            high(NP - 1, 0)
            high(NP - 1, 1)
            inverse(NP - 1)
            moments(NC - 1)

        @block.tensor
        def _(pe):
            pe.wait_ge(ident_set, 3)

            def turn_x(g, n, i):
                pe.wait_ge(x_in[n], 16 * i + 16)
                pe.wait_ge(xT_done, g)
                for k in range(KF):
                    for b in range(B):
                        ins = nc.tensor.transpose(acc[:, k, b * P:(b + 1) * P], xg[n][:, b, k * P:(k + 1) * P], ident[:, :])
                ins.then_inc(xTp_done, 1)

            def project(g, n):
                pe.wait_ge(xT_done, g + 1)
                pe.wait_ge(xt_kept, g)
                for b in range(B):
                    for k in range(KF):
                        ins = nc.tensor.matmul(acc[:, 2 + b, 0:WX], xT[n][:, k, b, :], Wx[:, k, :],
                                               start=(k == 0), stop=(k == KF - 1))
                ins.then_inc(xt_done, 1)

            turn_x(0, 0, 0)
            pe.wait_ge(wx_done, 2)
            with pe.Fori(0, NG // 2 - 1) as i:
                turn_x(2 * i + 1, 1, i)
                project(2 * i, 0)
                turn_x(2 * i + 2, 0, i + 1)
                project(2 * i + 1, 1)
            turn_x(NG - 1, 1, NG // 2 - 1)
            project(NG - 2, 0)
            project(NG - 1, 1)
            pe.wait_ge(xt_kept, NG)
            for h in range(H):
                ins = nc.tensor.transpose(spare[0:R, h * P:(h + 1) * P], tab[:, :, h], ident[:, :])
            ins.then_inc(sTp_done, 1)

            def turn_masks(k):
                pe.wait_ge(conv_done, 4 * k + 8)
                pe.wait_ge(at_done, k)
                for t in range(B):
                    ins = nc.tensor.transpose(tp[:, t * P:(t + 1) * P], nat[:, t, :].bitcast(fp32), ident[:, :])
                ins.then_inc(tp_done, 1)

            with pe.Fori(0, HALF) as k:
                turn_masks(k)

            def sums(P_, g, h, base, first):
                pe.wait_ge(pos_done, P_ * SP_ + 2 * g + h + 1)
                if first:
                    pe.wait_ge(u_done, 2 * P_ + h + 1)
                pe.sem_inc(pe_passed, 1)
                opened = set()
                for b in range(B):
                    for cd, m in ((0, pos), (1, neg)):
                        for t in range(B):
                            k, o = slot(t, cd)
                            opens = first and k not in opened
                            opened.add(k)
                            v = base + b * VW + h * HV + cd * 2 * VO
                            ins = nc.tensor.matmul(acc[:, 3 * h + k, o:o + 2 * VO], m[:, h, t * P:(t + 1) * P, b],
                                                   V[:, v:v + 2 * VO],
                                                   start=opens,
                                                   stop=False, skip_group_check=True)
                ins.then_inc(sums_done, 1)

            def one_pass(c, p, more):
                P_ = 2 * c + p
                for j in range(HALF):
                    if more:
                        turn_masks(P_ * HALF + HALF + j)
                    for g in (2 * j, 2 * j + 1):
                        for h in range(HP):
                            sums(P_, g, h, g * (B * VW) + p * (HP * HV), g == 0)

            with pe.Fori(0, NC - 1) as c:
                one_pass(c, 0, True)
                one_pass(c, 1, True)
            one_pass(NC - 1, 0, True)
            one_pass(NC - 1, 1, False)


_INS = ['x', 'adj', 'L0_gnn_W', 'L0_gnn_a']
_OUTS = [((8192, 256), 'float32')]


def kernel(**inputs):
    import numpy as _np
    import concourse.bacc as _bacc
    from concourse import mybir as _mybir
    from concourse.bass_utils import run_bass_kernel_spmd as _run

    nc = _bacc.Bacc("TRN2", target_bir_lowering=False, num_devices=1)
    arrays, args = {}, []
    for name in _INS:
        a = _np.ascontiguousarray(inputs[name])
        arrays[f"in_{name}_dram"] = a
        args.append(nc.dram_tensor(f"in_{name}_dram", a.shape, _mybir.dt.from_np(a.dtype), kind="ExternalInput").ap())
    for i, (shape, dtype) in enumerate(_OUTS):
        dt = _mybir.dt.from_np(_np.dtype(dtype))
        args.append(nc.dram_tensor(f"out_{i}_dram", shape, dt, kind="ExternalOutput").ap())
    gat_residual_norm(nc, *args)
    r = _run(nc, [arrays], core_ids=[0])
    return r.results[0]["out_0_dram"]
```

```python
import concourse.bass as bass
from concourse import mybir
from contextlib import ExitStack



def gat_residual_norm(nc: bass.Bass, x: bass.AP, adj: bass.AP, W: bass.AP, a: bass.AP, out: bass.AP):
    fp32 = mybir.dt.float32
    fp16 = mybir.dt.float16
    fp8 = mybir.dt.float8e4
    u32 = mybir.dt.uint32
    i32 = mybir.dt.int32
    i8 = mybir.dt.int8
    u8 = mybir.dt.uint8
    ALU = mybir.AluOpType
    ACT = mybir.ActivationFunctionType
    AX = mybir.AxisListType
    RMAX = bass.bass_isa.ReduceOp.max

    P = 128
    N, F = x.shape
    H, _, O = W.shape
    B = 4
    CW = B * P
    NC = N // CW
    NG = N // CW
    R = N // P
    KF = F // P
    VO = O + 1
    HV = 4 * VO
    VW = H * HV
    VX = VW // 2
    HP = 2
    NP = NC * (H // HP)
    WX = F + 2 * H
    SLOPE = 0.2
    EPS = 1e-5
    LOW = 2.0 ** 14
    SCALAR_BYTES = ((3, 3), (3, 2))
    assert N % CW == 0 and F == KF * P and H == 4 and H * O == F
    HALF = NG // 2
    STEPS = HP * NG

    ctx = ExitStack()
    with ctx:
        def sb(name, shape, dt):
            return ctx.enter_context(nc.sbuf_tensor(name, shape, dt))

        def sem(name):
            return ctx.enter_context(nc.semaphore(name))

        V = sb("V", [P, R * VW], fp16)
        V32 = V[:, :].bitcast(fp32)
        AT = sb("AT", [P, NG * CW], u32)
        raw = sb("raw", [P, B, CW], i32)
        nat = sb("nat", [P, B, CW], u8)
        srow = sb("srow", [P, 2, HP, CW], fp32)
        sgn = sb("sgn", [P, 2, HP, CW, B], i8)
        pos = sb("pos", [P, 2, HP, CW, B], fp8)
        u = sb("u", [P, HP, B, 2, VO], fp32)
        y = sb("y", [P, B, F], fp32)
        d_all = sb("d_all", [P, R, H], fp32)
        ab = sb("ab", [P, R, H, 2], fp32)
        ident = sb("ident", [P, P], fp32)
        mx = sb("mx", [P, H], fp32)
        M = sb("M", [P, H], fp32)
        rden = sb("rden", [P, HP, B], fp32)
        stats = sb("stats", [P, B, 6], fp32)
        mv = sb("mv", [P, B, 2], fp32)
        rstd = sb("rstd", [P, B], fp32)
        half = sb("half", [P, B], fp32)

        late = AT[:, HALF * CW:NG * CW].bitcast(fp32)
        xg = [late[:, n * B * F:(n + 1) * B * F].rearrange("p (b f) -> p b f", b=B) for n in range(2)]
        xT = [late[:, (2 + n) * B * F:(3 + n) * B * F].rearrange("p (k b q) -> p k b q", k=KF, b=B) for n in range(2)]
        UW = B * H * VO
        U1 = [late[:, n * UW:(n + 1) * UW].rearrange("p (r v) -> p r v", v=VO) for n in range(2)]
        scratch = [m.rearrange("p h i b -> p (h i b)").bitcast(fp32)
                 for m in (sgn[:, 0], pos[:, 0], pos[:, 1])]
        s_all = sgn[:, 1].rearrange("p h i b -> p (h i b)").bitcast(fp32)[:, 0:R * H].rearrange("p (r h) -> p r h", h=H)
        Wx = y[:, :, :].rearrange("p b f -> p (b f)")[:, 0:KF * WX].rearrange("p (k n) -> p k n", k=KF)
        aB = scratch[0][:, 0:H * 2 * O].rearrange("p (h n) -> p h n", h=H)
        prod = scratch[1][:, 0:KF * F].rearrange("p (k h o) -> p k h o", k=KF, h=H)
        dM = scratch[2][:, 0:R * H].rearrange("p (r h) -> p r h", h=H)
        tM = scratch[2][:, R * H:2 * R * H].rearrange("p (r h) -> p r h", h=H)
        tN = scratch[2][:, 2 * R * H:3 * R * H].rearrange("p (r h) -> p r h", h=H)
        tP = scratch[2][:, 3 * R * H:4 * R * H].rearrange("p (r h) -> p r h", h=H)
        e1 = dM
        e2 = y[:, :, :].rearrange("p b f -> p (b f)")[:, KF * WX:KF * WX + R * H].rearrange("p (r h) -> p r h", h=H)
        uall = u[:, :, :, :, :].rearrange("p h b c v -> p (h b c v)")
        U2 = [uall.rearrange("p (r v) -> p r v", v=VO), late[:, 2 * UW:3 * UW].rearrange("p (r v) -> p r v", v=VO)]
        sT = scratch[1][0:R, 0:H * P].rearrange("r (h p) -> r h p", h=H)

        acc = ctx.enter_context(nc.psum_tensor("acc", [P, 6, 512], fp32))
        tp = ctx.enter_context(nc.psum_tensor("tp", [P, 512], fp32))
        spare = ctx.enter_context(nc.psum_tensor("spare", [P, 512], fp32))

        s_dram = nc.dram_tensor("s_rows", [H, N], fp32, kind="Internal").ap()

        w_in = sem("w_in")
        a_in = sem("a_in")
        x_in = [sem("x_in0"), sem("x_in1")]
        ident_set = sem("ident_set")
        prod_done = sem("prod_done")
        wx_done = sem("wx_done")
        xTp_done = sem("xTp_done")
        xT_done = sem("xT_done")
        xt_done = sem("xt_done")
        xt_kept = sem("xt_kept")
        mx_done = sem("mx_done")
        M_done = sem("M_done")
        exp_in = sem("exp_in")
        exp_done = sem("exp_done")
        scaled = sem("scaled")
        sTp_done = sem("sTp_done")
        sT_done = sem("sT_done")
        s_out = sem("s_out")
        U1_done = sem("U1_done")
        U2_done = sem("U2_done")
        hi_done = sem("hi_done")
        lo_done = sem("lo_done")
        raw_in = [sem(f"raw_in{t}") for t in range(2)]
        conv_done = sem("conv_done")
        tp_done = sem("tp_done")
        at_done = sem("at_done")
        row_in = [[sem(f"row_in{q}{h}") for h in range(HP)] for q in range(2)]
        last_done = sem("last_done")
        sgn_done = sem("sgn_done")
        neg_done = sem("neg_done")
        pos_done = sem("pos_done")
        sums_done = sem("sums_done")
        low_done = sem("low_done")
        u_done = sem("u_done")
        wu_done = sem("wu_done")
        t_done = sem("t_done")
        rden_done = sem("rden_done")
        tr_done = sem("tr_done")
        y_done = sem("y_done")
        res_in = sem("res_in")
        stats_done = sem("stats_done")
        mv_done = sem("mv_done")
        pow_done = sem("pow_done")
        norm_done = sem("norm_done")
        out_done = sem("out_done")
        pe_passed = sem("pe_passed")
        pool_passed = sem("pool_passed")
        dve_passed = sem("dve_passed")

        block = ctx.enter_context(nc.Block())

        adj_v = adj.rearrange("(c p t) (g w) -> c g p t w", p=P, t=B, w=CW)
        x_v = x.rearrange("(g p b) f -> g p b f", p=P, b=B)
        out_v = out.rearrange("(g p b) f -> g p b f", p=P, b=B)
        s_v = s_dram.rearrange("h (c w) -> h c w", w=CW)

        sgn8 = sgn[:, :, :, :, :].bitcast(mybir.dt.float8e5)
        neg = sgn[:, :, :, :, :].bitcast(fp8)

        def word(t, d, h):
            return t[:, d, h].rearrange("p i b -> p (i b)").bitcast(u32)

        def slot(t, cd):
            q = t * 2 + cd
            return q // 3, (q % 3) * 2 * VO

        def xt_of(g):
            return V32[:, bass.ds(g * (B * VX), B * VX)].rearrange("p (b n) -> p b n", b=B)[:, :, 0:F] \
                .rearrange("p b (h o) -> p b h o", h=H)

        def e_of(e, g):
            return e[:, bass.ds(g * B, B), :].unsqueeze(3).broadcast_to([P, B, H, O])

        def e_flat(e, g):
            return e[:, bass.ds(g * B, B), :].rearrange("p b h -> p (b h)")

        def V_part(g, part):
            return V[:, bass.ds(g * (B * VW), B * VW)].rearrange("p (r n) -> p r n", n=HV)[:, :, part * VO:(part + 1) * VO]

        dflat = d_all[:, :, :].rearrange("p r h -> p (r h)")

        def acc_part(h, rect, part):
            if rect == 0:
                v = acc[:, 3 * h:3 * h + 2, 0:3 * 2 * VO].rearrange("p k (s n) -> p k s n", s=3)
                return v[:, :, :, part * VO:(part + 1) * VO]
            v = acc[:, 3 * h + 2, 0:2 * 2 * VO].rearrange("p (s n) -> p s n", s=2)
            return v[:, :, part * VO:(part + 1) * VO]


        @block.sync
        def _(sp):
            for k in range(KF):
                sp.dma_start(Wx[:, k, 0:F].rearrange("p (h o) -> p h o", h=H),
                             W[:, k * P:(k + 1) * P, :].rearrange("h p o -> p h o")).then_inc(w_in, 16)
            sp.dma_start(aB, a.rearrange("(q h) n -> q h n", q=1).broadcast_to([P, H, 2 * O])).then_inc(a_in, 16)

            def load(c, g, k):
                for t in range(2):
                    sp.wait_ge(conv_done, 2 * k + t + 1)
                    sp.dma_start(raw[:, 2 * t:2 * t + 2, :], adj_v[c, g, :, 2 * t:2 * t + 2, :]).then_inc(raw_in[t], 16)

            with sp.Fori(0, NG // 2) as i:
                for n in range(2):
                    sp.wait_ge(xTp_done, 2 * i + n + 1)
                    sp.dma_start(xg[n], x_v[2 * i + n]).then_inc(x_in[n], 16)
                load(0, i, i)

            def load_rows(c, p, q):
                for h in range(HP):
                    sp.dma_start(srow[:, q, h, :], s_v[HP * p + h, c].partition_broadcast(P)).then_inc(row_in[q][h], 16)

            sp.wait_ge(s_out, 16)
            load_rows(0, 0, 0)

            def one_pass(c, p):
                def group(j):
                    if p == 0:
                        load(c, HALF + j, NG * c + HALF + j)
                    else:
                        load(c + 1, j, NG * c + NG + j)

                group(0)
                sp.wait_ge(neg_done, (2 * c + p) * STEPS + 4)
                if p == 0:
                    load_rows(c, 1, 1)
                else:
                    load_rows(c + 1, 0, 0)
                with sp.Fori(1, HALF) as j:
                    group(j)

            with sp.Fori(0, NC - 1) as c:
                one_pass(c, 0)
                one_pass(c, 1)
            one_pass(NC - 1, 0)

        @block.gpsimd
        def _(pool):
            nc.gpsimd.memset(ident[:, :], 0.0).then_inc(ident_set, 1)
            pool.wait_ge(ident_set, 1)
            nc.gpsimd.affine_select(out=ident[:, :], in_=ident[:, :], compare_op=ALU.not_equal, fill=1.0,
                                    base=0, pattern=[[-1, P]], channel_multiplier=1).then_inc(ident_set, 1)
            nc.gpsimd.memset(half[:, :], -0.5).then_inc(ident_set, 1)
            pool.wait_ge(mx_done, 1)
            nc.gpsimd.partition_all_reduce(M[:, :], mx[:, :], P, RMAX).then_inc(M_done, 1)

            with pool.Fori(0, NG // 2) as i:
                for n in range(2):
                    g = 2 * i + n
                    pool.wait_ge(scaled, 2)
                    pool.wait_ge(lo_done, g + 1)
                    nc.gpsimd.tensor_tensor(
                        out=U2[n].rearrange("p (b h) v -> p b h v", b=B)[:, :, :, 0:O], in0=xt_of(g), in1=e_of(e2, g), op=ALU.mult).then_inc(U2_done, 1)
                    nc.gpsimd.tensor_copy(U2[n][:, :, O], e_flat(e2, g)).then_inc(U2_done, 1)

            def last_signs(pas, g, h, p):
                n = pas * STEPS + 2 * g + h
                pool.wait_ge(sums_done, n + 1)
                pool.sem_inc(pool_passed, 1)
                for b in range(SCALAR_BYTES[g % 2][h], B):
                    r = (g * B + b) * H + HP * p + h
                    ins = nc.gpsimd.tensor_tensor(out=sgn8[:, g % 2, h, :, b], in0=srow[:, p, h, :],
                                                  in1=dflat[:, r:r + 1].broadcast_to([P, CW]), op=ALU.add, saturate=False)
                ins.then_inc(last_done, 1)

            def weigh(c, p, last, h):
                pool.wait_ge(u_done, 2 * last + h + 3)
                w = ab[:, bass.ds(c * B, B), HP * p + h, :]
                nc.gpsimd.tensor_tensor(out=u[:, h], in0=u[:, h], in1=w.unsqueeze(3).broadcast_to([P, B, 2, VO]),
                                        op=ALU.mult).then_inc(wu_done, 1)

            def join(last, h):
                pool.wait_ge(wu_done, 2 * last + h + 1)
                nc.gpsimd.tensor_tensor(out=u[:, h, :, 0, :], in0=u[:, h, :, 0, :], in1=u[:, h, :, 1, :],
                                        op=ALU.add).then_inc(t_done, 1)

            def divide(last, h):
                pool.wait_ge(rden_done, last + 1)
                nc.gpsimd.tensor_tensor(out=u[:, h, :, 1, 0:O], in0=u[:, h, :, 0, 0:O],
                                        in1=rden[:, h, :].unsqueeze(2).broadcast_to([P, B, O]),
                                        op=ALU.mult).then_inc(tr_done, 1)

            def add_on(c, p, last, h):
                pool.wait_ge(res_in, 16 * c + 16)
                pool.wait_ge(tr_done, 2 * last + h + 1)
                yh = y[:, :, (HP * p + h) * O:(HP * p + h + 1) * O]
                nc.gpsimd.tensor_tensor(out=yh, in0=yh, in1=u[:, h, :, 1, 0:O], op=ALU.add).then_inc(y_done, 1)

            def deviation(c):
                pool.wait_ge(mv_done, c + 1)
                pool.sem_inc(pool_passed, 1)
                nc.gpsimd.tensor_scalar(rstd[:, :], mv[:, :, 1], EPS, None, ALU.add).then_inc(pow_done, 1)
                pool.wait_ge(pow_done, 2 * c + 1)
                nc.gpsimd.tensor_tensor(out=rstd[:, :], in0=rstd[:, :], in1=half[:, :], op=ALU.pow).then_inc(pow_done, 1)

            def normalise(c, t):
                pool.wait_ge(pow_done, 2 * c + 2)
                pool.sem_inc(pool_passed, 1)
                nc.gpsimd.tensor_scalar(y[:, t, :], y[:, t, :], mv[:, t, 0:1], rstd[:, t:t + 1],
                                        ALU.subtract, ALU.mult).then_inc(norm_done, 1)

            def store(c):
                pool.wait_ge(norm_done, B * c + B)
                pool.dma_start(out_v[c], y[:, :, :]).then_inc(out_done, 16)

            def load_res(c):
                pool.dma_start(y[:, :, :], x_v[c]).then_inc(res_in, 16)

            def one_pass(c, p, first=False, second=False):
                pas = 2 * c + p
                ec, ep, last = (c - 1, 1, pas - 1) if p == 0 else (c, 0, pas - 1)
                pool.wait_ge(row_in[p][0], 16 * c + 16)
                pool.wait_ge(row_in[p][1], 16 * c + 16)
                for g in range(NG):
                    for h in range(HP):
                        last_signs(pas, g, h, p)
                    if p == 1 and not second:
                        if g == 0:
                            deviation(c - 1)
                        if 1 <= g <= B:
                            normalise(c - 1, g - 1)
                        if g == B:
                            store(c - 1)
                    if p == 1 and g == 8:
                        if not second:
                            pool.wait_ge(out_done, 16 * c)
                        load_res(c)
                    if not first:
                        if g in (5, 7):
                            weigh(ec, ep, last, (g - 5) // 2)
                        if g in (6, 8):
                            join(last, (g - 6) // 2)
                        if g in (11, 13):
                            divide(last, (g - 11) // 2)
                        if g in (12, 14):
                            add_on(ec, ep, last, (g - 12) // 2)

            one_pass(0, 0, first=True)
            one_pass(0, 1, second=True)
            with pool.Fori(1, NC) as c:
                one_pass(c, 0)
                one_pass(c, 1)
            for h in range(HP):
                weigh(NC - 1, 1, NP - 1, h)
                join(NP - 1, h)
            for h in range(HP):
                divide(NP - 1, h)
                add_on(NC - 1, 1, NP - 1, h)
            deviation(NC - 1)
            for t in range(B):
                normalise(NC - 1, t)
            store(NC - 1)
            pool.wait_ge(out_done, 16 * NC)

        @block.scalar
        def _(act):
            with act.Fori(0, NG // 2) as i:
                for n in range(2):
                    g = 2 * i + n
                    act.wait_ge(xTp_done, g + 3)
                    act.wait_ge(xt_done, g + 1)
                    nc.scalar.activation(xT[n].rearrange("p k b q -> p (k b q)"),
                                         acc[:, 0:2, :].rearrange("p k n -> p (k n)"), ACT.Copy).then_inc(xT_done, 1)
            act.wait_ge(sTp_done, 1)
            act.wait_ge(wx_done, 2)
            nc.scalar.activation(sT.rearrange("r h p -> r (h p)"), spare[0:R, 0:H * P], ACT.Copy).then_inc(sT_done, 1)
            act.wait_ge(sT_done, 1)
            act.dma_start(s_dram.rearrange("h (r p) -> r h p", p=P), sT).then_inc(s_out, 16)
            act.wait_ge(exp_in, 4)
            nc.scalar.activation(e2, dM, ACT.Exp, scale=SLOPE).then_inc(exp_done, 1)
            act.wait_ge(exp_done, 1)
            nc.scalar.activation(e1, dM, ACT.Exp).then_inc(exp_done, 1)
            nc.scalar.activation(ab[:, :, :, 0], tN, ACT.Exp).then_inc(exp_done, 1)
            nc.scalar.activation(ab[:, :, :, 1], tP, ACT.Exp).then_inc(exp_done, 1)
            with act.Fori(0, NG // 2) as i:
                for n in range(2):
                    g = 2 * i + n
                    act.wait_ge(U1_done, 2 * g + 2)
                    act.wait_ge(U2_done, 2 * g + 2)
                    nc.scalar.activation(V_part(g, 0), U1[n], ACT.Copy, scale=1.0 / LOW).then_inc(hi_done, 1)
                    nc.scalar.activation(V_part(g, 2), U2[n], ACT.Copy, scale=1.0 / LOW).then_inc(hi_done, 1)

            def signs(pas, g, d, h, q):
                n = pas * STEPS + 2 * g + h
                act.wait_ge(sums_done, n + 1)
                for b in range(SCALAR_BYTES[d][h]):
                    r = (g * B + b) * H + q * HP + h
                    ins = nc.scalar.activation(sgn[:, d, h, :, b], srow[:, q, h, :], ACT.Sign,
                                               bias=dflat[:, bass.ds(r, 1)], scale=1.0)
                ins.then_inc(sgn_done, 1)

            def low(pas, h):
                act.wait_ge(sums_done, (pas + 1) * STEPS + h + 3)
                act.wait_ge(y_done, 2 * pas + h + 1)
                k0, k1 = (u[:, h].rearrange("p t c v -> p (t c) v")[:, 0:6, :], u[:, h].rearrange("p t c v -> p (t c) v")[:, 6:8, :])
                nc.scalar.activation(k0.rearrange("p (k s) v -> p k s v", k=2), acc_part(h, 0, 1), ACT.Copy, scale=1.0 / LOW)
                nc.scalar.activation(k1, acc_part(h, 1, 1), ACT.Copy, scale=1.0 / LOW).then_inc(low_done, 1)

            def one_pass(pas, c, q, first=False):
                act.wait_ge(row_in[q][0], 16 * c + 16)
                act.wait_ge(row_in[q][1], 16 * c + 16)
                signs(pas, 0, 0, 0, q)
                signs(pas, 0, 0, 1, q)
                if not first:
                    low(pas - 1, 0)
                signs(pas, 1, 1, 0, q)
                if not first:
                    low(pas - 1, 1)
                signs(pas, 1, 1, 1, q)
                with act.Fori(1, HALF) as j:
                    for d in range(2):
                        signs(pas, 2 * j + d, d, 0, q)
                        signs(pas, 2 * j + d, d, 1, q)

            one_pass(0, 0, 0, first=True)
            one_pass(1, 0, 1)
            with act.Fori(1, NC) as c:
                one_pass(2 * c, c, 0)
                one_pass(2 * c + 1, c, 1)
            low(NP - 1, 0)
            low(NP - 1, 1)

        @block.vector
        def _(dve):
            dve.sem_inc(xTp_done, 2)
            dve.sem_inc(xt_done, 2)
            dve.sem_inc(conv_done, 2)
            dve.sem_inc(neg_done, 4)
            dve.sem_inc(sums_done, 4)
            dve.sem_inc(u_done, 2)
            dve.sem_inc(y_done, 2)
            dve.sem_inc(lo_done, 2)
            dve.sem_inc(xt_kept, 1)
            dve.sem_inc(at_done, 1)
            dve.sem_inc(tp_done, 1)
            dve.sem_inc(xT_done, 1)
            dve.wait_ge(w_in, 16 * KF)
            dve.wait_ge(a_in, 16)
            wv = Wx[:, :, 0:F].rearrange("p k (h o) -> p k h o", h=H)
            for n in range(2):
                for k in range(KF):
                    if n and k == 0:
                        dve.wait_ge(wx_done, 1)
                    nc.vector.tensor_tensor(out=prod[:, k], in0=wv[:, k], in1=aB[:, :, n * O:(n + 1) * O],
                                            op=ALU.mult).then_inc(prod_done, 1)
                dve.wait_ge(prod_done, KF * (n + 1))
                nc.vector.tensor_reduce(Wx[:, :, F + n * H:F + (n + 1) * H], prod, AX.X, ALU.add).then_inc(wx_done, 1)

            def leave(g):
                dve.wait_ge(xt_done, g + 3)
                nc.vector.tensor_copy(
                    V32[:, bass.ds(g * (B * VX), B * VX)].rearrange("p (b n) -> p b n", b=B)[:, :, 0:F],
                    acc[:, 2:2 + B, 0:F])
                nc.vector.tensor_copy(s_all[:, bass.ds(g * B, B), :], acc[:, 2:2 + B, F:F + H])
                nc.vector.tensor_copy(d_all[:, bass.ds(g * B, B), :], acc[:, 2:2 + B, F + H:WX]).then_inc(xt_kept, 1)

            def keep(g, k):
                dve.wait_ge(tp_done, k + 2)
                nc.vector.tensor_scalar(AT[:, bass.ds(g * CW, CW)], tp[:, :].bitcast(u32), 0x10101010, 2,
                                        ALU.bitwise_and, ALU.logical_shift_left).then_inc(at_done, 1)

            def convert(k, ts):
                for t in ts:
                    dve.wait_ge(raw_in[t], 16 * k + 16)
                    dve.wait_ge(tp_done, k + 1)
                    nc.vector.tensor_scalar(nat[:, 2 * t:2 * t + 2, :], raw[:, 2 * t:2 * t + 2, :],
                                            0.0, 15.0, ALU.is_gt, ALU.add).then_inc(conv_done, 1)

            convert(0, range(2))
            with dve.Fori(0, HALF - 1) as i:
                leave(2 * i)
                keep(i, i)
                leave(2 * i + 1)
                convert(i + 1, range(2))
            leave(NG - 2)
            leave(NG - 1)
            dve.wait_ge(xt_kept, NG + 1)
            nc.vector.tensor_reduce(mx[:, :], d_all[:, :, :].rearrange("p r h -> p h r"), AX.X, ALU.max).then_inc(mx_done, 1)
            keep(HALF - 1, HALF - 1)
            dve.wait_ge(M_done, 1)
            Mb = M[:, :].unsqueeze(1).broadcast_to([P, R, H])
            nc.vector.tensor_tensor(out=dM, in0=d_all[:, :, :], in1=Mb, op=ALU.subtract).then_inc(exp_in, 1)
            nc.vector.tensor_tensor(out=tM, in0=s_all, in1=Mb, op=ALU.add).then_inc(exp_in, 1)
            dve.wait_ge(exp_in, 2)
            nc.vector.tensor_scalar(tN, tM, 1.0 - SLOPE, 0.0, ALU.mult, ALU.min).then_inc(exp_in, 1)
            nc.vector.tensor_scalar(tP, tM, SLOPE - 1.0, 0.0, ALU.mult, ALU.min).then_inc(exp_in, 1)
            dve.wait_ge(exp_done, 4)
            nc.vector.tensor_scalar(e1, e1, LOW, None, ALU.mult).then_inc(scaled, 1)
            nc.vector.tensor_scalar(e2, e2, LOW, None, ALU.mult).then_inc(scaled, 1)
            dve.wait_ge(scaled, 2)

            def table1(g, n):
                nc.vector.tensor_tensor(out=U1[n].rearrange("p (b h) v -> p b h v", b=B)[:, :, :, 0:O],
                                        in0=xt_of(g), in1=e_of(e1, g), op=ALU.mult).then_inc(U1_done, 1)
                nc.vector.tensor_copy(U1[n][:, :, O], e_flat(e1, g)).then_inc(U1_done, 1)

            def lows(g, n):
                dve.wait_ge(hi_done, 2 * g + 2)
                nc.vector.scalar_tensor_tensor(out=V_part(g, 1), in0=V_part(g, 0), scalar=-LOW, in1=U1[n],
                                               op0=ALU.mult, op1=ALU.add)
                nc.vector.scalar_tensor_tensor(out=V_part(g, 3), in0=V_part(g, 2), scalar=-LOW, in1=U2[n],
                                               op0=ALU.mult, op1=ALU.add).then_inc(lo_done, 1)

            table1(0, 0)
            with dve.Fori(0, HALF - 1) as i:
                table1(2 * i + 1, 1)
                lows(2 * i, 0)
                dve.wait_ge(lo_done, 2 * i + 3)
                table1(2 * i + 2, 0)
                lows(2 * i + 1, 1)
                dve.wait_ge(lo_done, 2 * i + 4)
            table1(NG - 1, 1)
            lows(NG - 2, 0)
            lows(NG - 1, 1)
            convert(HALF, range(2))
            dve.wait_ge(lo_done, NG + 2)
            dve.wait_ge(s_out, 16)

            def masks_of(pas, g, d, h, q):
                n = pas * STEPS + 2 * g + h
                at = AT[:, bass.ds(g * CW, CW)]
                dve.wait_ge(at_done, (pas * HALF if q == 0 else (pas - 1) * HALF) + g + 2)
                dve.wait_ge(last_done, n + 1)
                dve.wait_ge(sgn_done, n + 1)
                dve.wait_ge(sums_done, n + 1)
                nc.vector.scalar_tensor_tensor(out=word(sgn, d, h), in0=word(sgn, d, h), scalar=1, in1=at,
                                               op0=ALU.logical_shift_right, op1=ALU.bitwise_and).then_inc(neg_done, 1)

            def rest_of(pas, g, d, h):
                n = pas * STEPS + 2 * g + h
                dve.wait_ge(neg_done, n + 5)
                nc.vector.tensor_tensor(out=word(pos, d, h), in0=AT[:, bass.ds(g * CW, CW)], in1=word(sgn, d, h),
                                        op=ALU.bitwise_xor).then_inc(pos_done, 1)

            def high(pas, h):
                dve.wait_ge(low_done, 2 * pas + h + 1)
                uv = u[:, h].rearrange("p t c v -> p (t c) v")
                k0 = uv[:, 0:6, :].rearrange("p (k s) v -> p k s v", k=2)
                nc.vector.tensor_tensor(out=k0, in0=k0, in1=acc_part(h, 0, 0), op=ALU.add)
                nc.vector.tensor_tensor(out=uv[:, 6:8, :], in0=uv[:, 6:8, :], in1=acc_part(h, 1, 0),
                                        op=ALU.add).then_inc(u_done, 1)

            def two_groups(pas, j, q, more, last=None, ahead=True):
                k = pas * HALF + HALF + j
                for d in range(2):
                    g = 2 * j + d
                    for h in range(HP):
                        masks_of(pas, g, d, h, q)
                        rest_of(pas, g, d, h)
                        if last is not None and d == 0:
                            high(last, h)
                        if more and 2 * d + h == 1:
                            dve.wait_ge(pos_done, pas * STEPS + 4 * j + 2)
                            keep(j if q == 1 else j + HALF, k)
                        if more and ahead and 2 * d + h >= 2:
                            convert(k + 1, (2 * d + h - 2,))

            def inverse(last):
                dve.wait_ge(t_done, 2 * last + 2)
                dve.wait_ge(y_done, 2 * last + 2)
                nc.vector.reciprocal(rden[:, :, :], u[:, :, :, 0, O]).then_inc(rden_done, 1)

            def moments(c):
                dve.wait_ge(y_done, 4 * c + 6)
                for t in range(B):
                    nc.vector.bn_stats(stats[:, t, :], y[:, t, :]).then_inc(stats_done, 1)
                dve.wait_ge(stats_done, B * c + B)
                dve.sem_inc(dve_passed, 1)
                for t in range(B):
                    ins = nc.vector.bn_aggr(mv[:, t, :], stats[:, t, :])
                ins.then_inc(mv_done, 1)

            def one_pass(pas, c, q, first=False, more=True, ends=False):
                two_groups(pas, 0, q, more, None if first else pas - 1)
                with dve.Fori(1, 5) as j:
                    two_groups(pas, j, q, more)
                if not first:
                    inverse(pas - 1)
                with dve.Fori(5, HALF - 1 if ends else HALF) as j:
                    two_groups(pas, j, q, more)
                if ends:
                    two_groups(pas, HALF - 1, q, more, ahead=False)
                if q == 0 and not first:
                    moments(c - 1)

            one_pass(0, 0, 0, first=True)
            one_pass(1, 0, 1)
            with dve.Fori(1, NC - 1) as c:
                one_pass(2 * c, c, 0)
                one_pass(2 * c + 1, c, 1)
            one_pass(NP - 2, NC - 1, 0, ends=True)
            one_pass(NP - 1, NC - 1, 1, more=False)
            high(NP - 1, 0)
            high(NP - 1, 1)
            inverse(NP - 1)
            moments(NC - 1)

        @block.tensor
        def _(pe):
            pe.wait_ge(ident_set, 3)

            def turn_x(g, n, i):
                pe.wait_ge(x_in[n], 16 * i + 16)
                pe.wait_ge(xT_done, g + 1)
                for k in range(KF):
                    for b in range(B):
                        ins = nc.tensor.transpose(acc[:, k, b * P:(b + 1) * P], xg[n][:, b, k * P:(k + 1) * P], ident[:, :])
                ins.then_inc(xTp_done, 1)

            def project(g, n):
                pe.wait_ge(xT_done, g + 2)
                pe.wait_ge(xt_kept, g + 1)
                for b in range(B):
                    for k in range(KF):
                        ins = nc.tensor.matmul(acc[:, 2 + b, 0:WX], xT[n][:, k, b, :], Wx[:, k, :],
                                               start=(k == 0), stop=(k == KF - 1))
                ins.then_inc(xt_done, 1)

            def turn_masks(k):
                pe.wait_ge(conv_done, 2 * k + 4)
                pe.wait_ge(at_done, k + 1)
                for t in range(B):
                    ins = nc.tensor.transpose(tp[:, t * P:(t + 1) * P], nat[:, t, :].bitcast(fp32), ident[:, :])
                ins.then_inc(tp_done, 1)

            turn_x(0, 0, 0)
            pe.wait_ge(wx_done, 2)
            with pe.Fori(0, NG // 2 - 1) as i:
                turn_x(2 * i + 1, 1, i)
                project(2 * i, 0)
                turn_masks(i)
                turn_x(2 * i + 2, 0, i + 1)
                project(2 * i + 1, 1)
            turn_x(NG - 1, 1, NG // 2 - 1)
            project(NG - 2, 0)
            project(NG - 1, 1)
            pe.wait_ge(xt_kept, NG + 1)
            for h in range(H):
                ins = nc.tensor.transpose(spare[0:R, h * P:(h + 1) * P], s_all[:, :, h], ident[:, :])
            ins.then_inc(sTp_done, 1)
            turn_masks(HALF - 1)

            def sums(pas, g, h, base, first):
                pe.wait_ge(pos_done, pas * STEPS + 2 * g + h + 1)
                if first:
                    pe.wait_ge(u_done, 2 * pas + h + 1)
                pe.sem_inc(pe_passed, 1)
                opened = set()
                for b in range(B):
                    for cd, m in ((0, pos), (1, neg)):
                        for t in range(B):
                            k, o = slot(t, cd)
                            opens = first and k not in opened
                            opened.add(k)
                            v = base + b * VW + h * HV + cd * 2 * VO
                            ins = nc.tensor.matmul(acc[:, 3 * h + k, o:o + 2 * VO], m[:, g % 2, h, t * P:(t + 1) * P, b],
                                                   V[:, v:v + 2 * VO],
                                                   start=opens,
                                                   stop=False, skip_group_check=True)
                ins.then_inc(sums_done, 1)

            def one_pass(c, p, more, ends=False):
                pas = 2 * c + p
                for j in range(HALF):
                    for g in (2 * j, 2 * j + 1):
                        for h in range(HP):
                            if g % 2 == 0 and h == 0 and more:
                                turn_masks(pas * HALF + HALF + j)
                            sums(pas, g, h, g * (B * VW) + p * (HP * HV), g == 0)

            with pe.Fori(0, NC - 1) as c:
                one_pass(c, 0, True)
                one_pass(c, 1, True)
            one_pass(NC - 1, 0, True, ends=True)
            one_pass(NC - 1, 1, False)


_INS = ['x', 'adj', 'L0_gnn_W', 'L0_gnn_a']
_OUTS = [((8192, 256), 'float32')]


def kernel(**inputs):
    import numpy as _np
    import concourse.bacc as _bacc
    from concourse import mybir as _mybir
    from concourse.bass_utils import run_bass_kernel_spmd as _run

    nc = _bacc.Bacc("TRN2", target_bir_lowering=False, num_devices=1)
    arrays, args = {}, []
    for name in _INS:
        a = _np.ascontiguousarray(inputs[name])
        arrays[f"in_{name}_dram"] = a
        args.append(nc.dram_tensor(f"in_{name}_dram", a.shape, _mybir.dt.from_np(a.dtype), kind="ExternalInput").ap())
    for i, (shape, dtype) in enumerate(_OUTS):
        dt = _mybir.dt.from_np(_np.dtype(dtype))
        args.append(nc.dram_tensor(f"out_{i}_dram", shape, dt, kind="ExternalOutput").ap())
    gat_residual_norm(nc, *args)
    r = _run(nc, [arrays], core_ids=[0])
    return r.results[0]["out_0_dram"]
```
